# Optimizing a Trainium2 kernel written in Bass

```python
import numpy as np
import jax
import jax.numpy as jnp

def _softmax(x, axis=-1):
    return jax.nn.softmax(x, axis=axis)

def _gelu(x):
    return jax.nn.gelu(x, approximate=True)

def _silu(x):
    return jax.nn.silu(x)

def _sigmoid(x):
    return jax.nn.sigmoid(x)

def _layernorm(x, axis=-1, eps=1e-05):
    m = jnp.mean(x, axis=axis, keepdims=True)
    v = jnp.var(x, axis=axis, keepdims=True)
    return (x - m) / jnp.sqrt(v + eps)

def _scatter_add(tgt, idx, src, axis=0):
    return tgt.at[idx].add(src)

def _segment_sum(src, seg, n):
    return jax.ops.segment_sum(src, seg, n)
kernel_name = 'mk_seq_postln_d1_jaxref_r4_a2bf65'

def setup_inputs(seed: int=0):
    np.random.seed(seed)
    _w = jnp.asarray

    def _L0_attn_setup():
        import jax, jax.numpy as jnp
        import numpy as np
        B, T, NE, H = (4, 256, 256, 16)
        HS = NE // H
        EPS = 0.00064

        def _forward(x, time_maa_x, time_maa, maa_w1, maa_w2, decay_w1, decay_w2, aaa_w1, aaa_w2, kkk_w1, kkk_w2, gate_w1, gate_w2, ma_w1, ma_w2, mk_w1, mk_w2, time_decay, time_faaaa, time_aaaaa, time_misc_a, time_misc_k, Wr, Wk, Wv, Wo, ln_w, ln_b):
            Bx, Tx, C = x.shape
            xx = jnp.pad(x, ((0, 0), (1, 0), (0, 0)))[:, :Tx] - x
            mix = x + xx * time_maa_x
            lo = jnp.tanh(jnp.einsum('btc,dc->btd', mix, maa_w1)).reshape(Bx, Tx, 4, 32)
            lo = jnp.einsum('btgk,gkc->gbtc', lo, maa_w2)
            xm = x[None] + xx[None] * (lo + time_maa)
            xrg, xwa, xk, xv = (xm[0], xm[1], xm[2], xm[3])
            r = xrg @ Wr.T
            g = jnp.tanh(xrg @ gate_w1.T) @ gate_w2
            k = xk @ Wk.T
            v = xv @ Wv.T
            w2 = jnp.tanh(xwa @ decay_w1.T) @ decay_w2
            w = -jax.nn.softplus(-(time_decay + w2)) - 0.5
            kk = k + jnp.tanh(xk @ kkk_w1.T) @ kkk_w2
            kkh = kk.reshape(Bx, Tx, H, HS)
            kk = (kkh / jnp.maximum(jnp.linalg.norm(kkh, axis=-1, keepdims=True), 1e-12)).reshape(Bx, Tx, C)
            a = jax.nn.sigmoid(time_aaaaa + xwa @ aaa_w1.T @ aaa_w2)
            ma = jax.nn.sigmoid(time_misc_a + xwa @ ma_w1.T @ ma_w2)
            k = k * ma + k * a * (1.0 - ma)
            mk = jax.nn.sigmoid(time_misc_k + xk @ mk_w1.T @ mk_w2)
            k = k * jnp.exp(w * mk)
            b = -kk * a

            def to_th(t):
                return t.reshape(Bx, Tx, H, HS).transpose(1, 0, 2, 3)
            qt, wt, kt, vt, at, bt = map(to_th, (r, w, k, v, kk, b))
            wt = jnp.exp(-jnp.exp(wt))

            def step(s, inp):
                q_, w_, k_, v_, a_, b_ = inp
                sa = jnp.einsum('bhij,bhj->bhi', s, a_)
                s = s * w_[:, :, None, :] + sa[..., None] * b_[:, :, None, :] + v_[..., None] * k_[:, :, None, :]
                return (s, jnp.einsum('bhij,bhj->bhi', s, q_))
            s0 = jnp.zeros((Bx, H, HS, HS), x.dtype)
            _, y = jax.lax.scan(step, s0, (qt, wt, kt, vt, at, bt))
            y = y.transpose(1, 0, 2, 3).reshape(Bx, Tx, C)
            yg = y.reshape(Bx, Tx, H, HS)
            mu = yg.mean(-1, keepdims=True)
            var = ((yg - mu) ** 2).mean(-1, keepdims=True)
            y = ((yg - mu) / jnp.sqrt(var + EPS)).reshape(Bx, Tx, C) * ln_w + ln_b
            rk = (r.reshape(Bx, Tx, H, HS) * k.reshape(Bx, Tx, H, HS) * time_faaaa.reshape(H, HS)).sum(-1, keepdims=True)
            y = y + (rk * v.reshape(Bx, Tx, H, HS)).reshape(Bx, Tx, C)
            return y * g @ Wo.T
        key = jax.random.key(seed)
        ks = jax.random.split(key, 30)

        def rn(k, shape, s):
            return jax.random.normal(k, shape, jnp.float32) * s
        d = {}
        d['x'] = jax.random.normal(ks[0], (B, T, NE), jnp.float32)
        d['time_maa_x'] = jax.random.uniform(ks[1], (NE,), jnp.float32)
        d['time_maa'] = jax.random.uniform(ks[2], (4, 1, 1, NE), jnp.float32)
        d['maa_w1'] = rn(ks[3], (128, NE), 0.02)
        d['maa_w2'] = rn(ks[4], (4, 32, NE), 0.02)
        d['decay_w1'] = rn(ks[5], (64, NE), 0.02)
        d['decay_w2'] = rn(ks[6], (64, NE), 0.02)
        d['aaa_w1'] = rn(ks[7], (16, NE), 0.02)
        d['aaa_w2'] = rn(ks[8], (16, NE), 0.02)
        d['kkk_w1'] = rn(ks[9], (16, NE), 0.02)
        d['kkk_w2'] = rn(ks[10], (16, NE), 0.02)
        d['gate_w1'] = rn(ks[11], (128, NE), 0.02)
        d['gate_w2'] = rn(ks[12], (128, NE), 0.02)
        d['ma_w1'] = rn(ks[13], (16, NE), 0.02)
        d['ma_w2'] = rn(ks[14], (16, NE), 0.02)
        d['mk_w1'] = rn(ks[15], (16, NE), 0.02)
        d['mk_w2'] = rn(ks[16], (16, NE), 0.02)
        d['time_decay'] = jnp.linspace(-6.5, -1.5, NE, dtype=jnp.float32)
        d['time_faaaa'] = rn(ks[17], (NE,), 0.02)
        d['time_aaaaa'] = rn(ks[18], (NE,), 0.02)
        d['time_misc_a'] = rn(ks[19], (NE,), 0.02)
        d['time_misc_k'] = rn(ks[20], (NE,), 0.02)
        d['Wr'] = rn(ks[21], (NE, NE), 0.5 / NE ** 0.5)
        d['Wk'] = rn(ks[22], (NE, NE), 0.05 / NE ** 0.5)
        d['Wv'] = rn(ks[23], (NE, NE), 0.5 / NE ** 0.5)
        d['Wo'] = rn(ks[24], (NE, NE), 1.0 / NE ** 0.5)
        d['ln_w'] = jnp.ones((NE,), jnp.float32)
        d['ln_b'] = jnp.zeros((NE,), jnp.float32)
        return d
    _L0_attn_in = _L0_attn_setup()

    def _L0_ffn_setup():
        import jax, jax.numpy as jnp
        import numpy as np
        E = 8
        D = 256
        F = 1024
        S, B = (512, 2)
        LN_EPS = 1e-05

        def _moe_forward(input_features, centroids, ln_g, ln_b, W1, b1, W2, b2):
            s, b, d = input_features.shape
            x = jnp.swapaxes(input_features, 0, 1).reshape(-1, d)
            logits = x.astype(jnp.float32) @ centroids.astype(jnp.float32).T
            assign = jnp.argmax(logits, axis=-1)
            onehot = jax.nn.one_hot(assign, E, dtype=x.dtype)
            disp = jnp.einsum('te,td->etd', onehot, x)
            mu = disp.mean(-1, keepdims=True)
            var = disp.var(-1, keepdims=True)
            xn = (disp - mu) * jax.lax.rsqrt(var + LN_EPS)
            xn = xn * ln_g[:, None, :] + ln_b[:, None, :]
            h = jax.nn.relu(jnp.einsum('etd,edf->etf', xn, W1) + b1[:, None, :])
            y = jnp.einsum('etf,efd->etd', h, W2) + b2[:, None, :]
            y = disp + y
            out = jnp.einsum('te,etd->td', onehot, y)
            return jnp.swapaxes(out.reshape(b, s, d), 0, 1)
        key = jax.random.key(seed)
        ks = jax.random.split(key, 8)
        scale_in = 1.0 / np.sqrt(D)
        scale_ff = 1.0 / np.sqrt(F)
        return {'input_features': jax.random.normal(ks[0], (S, B, D), dtype=jnp.float32), 'centroids': jax.random.normal(ks[1], (E, D), dtype=jnp.float32) * scale_in, 'ln_g': jnp.ones((E, D), dtype=jnp.float32), 'ln_b': jnp.zeros((E, D), dtype=jnp.float32), 'W1': jax.random.normal(ks[2], (E, D, F), dtype=jnp.float32) * scale_in, 'b1': jax.random.normal(ks[3], (E, F), dtype=jnp.float32) * 0.01, 'W2': jax.random.normal(ks[4], (E, F, D), dtype=jnp.float32) * scale_ff, 'b2': jax.random.normal(ks[5], (E, D), dtype=jnp.float32) * 0.01}
    _L0_ffn_in = _L0_ffn_setup()
    _d = {'L0_attn_x': _L0_attn_in['x'], 'L0_attn_time_maa_x': _L0_attn_in['time_maa_x'], 'L0_attn_time_maa': _L0_attn_in['time_maa'], 'L0_attn_maa_w1': _L0_attn_in['maa_w1'], 'L0_attn_maa_w2': _L0_attn_in['maa_w2'], 'L0_attn_decay_w1': _L0_attn_in['decay_w1'], 'L0_attn_decay_w2': _L0_attn_in['decay_w2'], 'L0_attn_aaa_w1': _L0_attn_in['aaa_w1'], 'L0_attn_aaa_w2': _L0_attn_in['aaa_w2'], 'L0_attn_kkk_w1': _L0_attn_in['kkk_w1'], 'L0_attn_kkk_w2': _L0_attn_in['kkk_w2'], 'L0_attn_gate_w1': _L0_attn_in['gate_w1'], 'L0_attn_gate_w2': _L0_attn_in['gate_w2'], 'L0_attn_ma_w1': _L0_attn_in['ma_w1'], 'L0_attn_ma_w2': _L0_attn_in['ma_w2'], 'L0_attn_mk_w1': _L0_attn_in['mk_w1'], 'L0_attn_mk_w2': _L0_attn_in['mk_w2'], 'L0_attn_time_decay': _L0_attn_in['time_decay'], 'L0_attn_time_faaaa': _L0_attn_in['time_faaaa'], 'L0_attn_time_aaaaa': _L0_attn_in['time_aaaaa'], 'L0_attn_time_misc_a': _L0_attn_in['time_misc_a'], 'L0_attn_time_misc_k': _L0_attn_in['time_misc_k'], 'L0_attn_Wr': _L0_attn_in['Wr'], 'L0_attn_Wk': _L0_attn_in['Wk'], 'L0_attn_Wv': _L0_attn_in['Wv'], 'L0_attn_Wo': _L0_attn_in['Wo'], 'L0_attn_ln_w': _L0_attn_in['ln_w'], 'L0_attn_ln_b': _L0_attn_in['ln_b'], 'L0_ffn_centroids': _L0_ffn_in['centroids'], 'L0_ffn_ln_g': _L0_ffn_in['ln_g'], 'L0_ffn_ln_b': _L0_ffn_in['ln_b'], 'L0_ffn_W1': _L0_ffn_in['W1'], 'L0_ffn_b1': _L0_ffn_in['b1'], 'L0_ffn_W2': _L0_ffn_in['W2'], 'L0_ffn_b2': _L0_ffn_in['b2']}
    _x0 = _d['L0_attn_x']
    _d['L0_attn_x'] = jax.random.normal(jax.random.fold_in(jax.random.key(seed), 1), (8, 512, 256), dtype=_x0.dtype)
    del _x0
    return _d

def reference(L0_attn_x, L0_attn_time_maa_x, L0_attn_time_maa, L0_attn_maa_w1, L0_attn_maa_w2, L0_attn_decay_w1, L0_attn_decay_w2, L0_attn_aaa_w1, L0_attn_aaa_w2, L0_attn_kkk_w1, L0_attn_kkk_w2, L0_attn_gate_w1, L0_attn_gate_w2, L0_attn_ma_w1, L0_attn_ma_w2, L0_attn_mk_w1, L0_attn_mk_w2, L0_attn_time_decay, L0_attn_time_faaaa, L0_attn_time_aaaaa, L0_attn_time_misc_a, L0_attn_time_misc_k, L0_attn_Wr, L0_attn_Wk, L0_attn_Wv, L0_attn_Wo, L0_attn_ln_w, L0_attn_ln_b, L0_ffn_centroids, L0_ffn_ln_g, L0_ffn_ln_b, L0_ffn_W1, L0_ffn_b1, L0_ffn_W2, L0_ffn_b2):

    def _L0_attn_ref(x, time_maa_x, time_maa, maa_w1, maa_w2, decay_w1, decay_w2, aaa_w1, aaa_w2, kkk_w1, kkk_w2, gate_w1, gate_w2, ma_w1, ma_w2, mk_w1, mk_w2, time_decay, time_faaaa, time_aaaaa, time_misc_a, time_misc_k, Wr, Wk, Wv, Wo, ln_w, ln_b):
        import jax, jax.numpy as jnp
        import numpy as np
        B, T, NE, H = (4, 256, 256, 16)
        HS = NE // H
        EPS = 0.00064

        def _forward(x, time_maa_x, time_maa, maa_w1, maa_w2, decay_w1, decay_w2, aaa_w1, aaa_w2, kkk_w1, kkk_w2, gate_w1, gate_w2, ma_w1, ma_w2, mk_w1, mk_w2, time_decay, time_faaaa, time_aaaaa, time_misc_a, time_misc_k, Wr, Wk, Wv, Wo, ln_w, ln_b):
            Bx, Tx, C = x.shape
            xx = jnp.pad(x, ((0, 0), (1, 0), (0, 0)))[:, :Tx] - x
            mix = x + xx * time_maa_x
            lo = jnp.tanh(jnp.einsum('btc,dc->btd', mix, maa_w1)).reshape(Bx, Tx, 4, 32)
            lo = jnp.einsum('btgk,gkc->gbtc', lo, maa_w2)
            xm = x[None] + xx[None] * (lo + time_maa)
            xrg, xwa, xk, xv = (xm[0], xm[1], xm[2], xm[3])
            r = xrg @ Wr.T
            g = jnp.tanh(xrg @ gate_w1.T) @ gate_w2
            k = xk @ Wk.T
            v = xv @ Wv.T
            w2 = jnp.tanh(xwa @ decay_w1.T) @ decay_w2
            w = -jax.nn.softplus(-(time_decay + w2)) - 0.5
            kk = k + jnp.tanh(xk @ kkk_w1.T) @ kkk_w2
            kkh = kk.reshape(Bx, Tx, H, HS)
            kk = (kkh / jnp.maximum(jnp.linalg.norm(kkh, axis=-1, keepdims=True), 1e-12)).reshape(Bx, Tx, C)
            a = jax.nn.sigmoid(time_aaaaa + xwa @ aaa_w1.T @ aaa_w2)
            ma = jax.nn.sigmoid(time_misc_a + xwa @ ma_w1.T @ ma_w2)
            k = k * ma + k * a * (1.0 - ma)
            mk = jax.nn.sigmoid(time_misc_k + xk @ mk_w1.T @ mk_w2)
            k = k * jnp.exp(w * mk)
            b = -kk * a

            def to_th(t):
                return t.reshape(Bx, Tx, H, HS).transpose(1, 0, 2, 3)
            qt, wt, kt, vt, at, bt = map(to_th, (r, w, k, v, kk, b))
            wt = jnp.exp(-jnp.exp(wt))

            def step(s, inp):
                q_, w_, k_, v_, a_, b_ = inp
                sa = jnp.einsum('bhij,bhj->bhi', s, a_)
                s = s * w_[:, :, None, :] + sa[..., None] * b_[:, :, None, :] + v_[..., None] * k_[:, :, None, :]
                return (s, jnp.einsum('bhij,bhj->bhi', s, q_))
            s0 = jnp.zeros((Bx, H, HS, HS), x.dtype)
            _, y = jax.lax.scan(step, s0, (qt, wt, kt, vt, at, bt))
            y = y.transpose(1, 0, 2, 3).reshape(Bx, Tx, C)
            yg = y.reshape(Bx, Tx, H, HS)
            mu = yg.mean(-1, keepdims=True)
            var = ((yg - mu) ** 2).mean(-1, keepdims=True)
            y = ((yg - mu) / jnp.sqrt(var + EPS)).reshape(Bx, Tx, C) * ln_w + ln_b
            rk = (r.reshape(Bx, Tx, H, HS) * k.reshape(Bx, Tx, H, HS) * time_faaaa.reshape(H, HS)).sum(-1, keepdims=True)
            y = y + (rk * v.reshape(Bx, Tx, H, HS)).reshape(Bx, Tx, C)
            return y * g @ Wo.T
        return _forward(x, time_maa_x, time_maa, maa_w1, maa_w2, decay_w1, decay_w2, aaa_w1, aaa_w2, kkk_w1, kkk_w2, gate_w1, gate_w2, ma_w1, ma_w2, mk_w1, mk_w2, time_decay, time_faaaa, time_aaaaa, time_misc_a, time_misc_k, Wr, Wk, Wv, Wo, ln_w, ln_b)

    def _L0_ffn_ref(input_features, centroids, ln_g, ln_b, W1, b1, W2, b2):
        import jax, jax.numpy as jnp
        import numpy as np
        E = 8
        D = 256
        F = 1024
        S, B = (512, 2)
        LN_EPS = 1e-05

        def _moe_forward(input_features, centroids, ln_g, ln_b, W1, b1, W2, b2):
            s, b, d = input_features.shape
            x = jnp.swapaxes(input_features, 0, 1).reshape(-1, d)
            logits = x.astype(jnp.float32) @ centroids.astype(jnp.float32).T
            assign = jnp.argmax(logits, axis=-1)
            onehot = jax.nn.one_hot(assign, E, dtype=x.dtype)
            disp = jnp.einsum('te,td->etd', onehot, x)
            mu = disp.mean(-1, keepdims=True)
            var = disp.var(-1, keepdims=True)
            xn = (disp - mu) * jax.lax.rsqrt(var + LN_EPS)
            xn = xn * ln_g[:, None, :] + ln_b[:, None, :]
            h = jax.nn.relu(jnp.einsum('etd,edf->etf', xn, W1) + b1[:, None, :])
            y = jnp.einsum('etf,efd->etd', h, W2) + b2[:, None, :]
            y = disp + y
            out = jnp.einsum('te,etd->td', onehot, y)
            return jnp.swapaxes(out.reshape(b, s, d), 0, 1)
        return _moe_forward(input_features, centroids, ln_g, ln_b, W1, b1, W2, b2)
    x = L0_attn_x
    x = _layernorm(x + _L0_attn_ref(x, L0_attn_time_maa_x, L0_attn_time_maa, L0_attn_maa_w1, L0_attn_maa_w2, L0_attn_decay_w1, L0_attn_decay_w2, L0_attn_aaa_w1, L0_attn_aaa_w2, L0_attn_kkk_w1, L0_attn_kkk_w2, L0_attn_gate_w1, L0_attn_gate_w2, L0_attn_ma_w1, L0_attn_ma_w2, L0_attn_mk_w1, L0_attn_mk_w2, L0_attn_time_decay, L0_attn_time_faaaa, L0_attn_time_aaaaa, L0_attn_time_misc_a, L0_attn_time_misc_k, L0_attn_Wr, L0_attn_Wk, L0_attn_Wv, L0_attn_Wo, L0_attn_ln_w, L0_attn_ln_b), axis=-1)
    x = _layernorm(x + _L0_ffn_ref(x, L0_ffn_centroids, L0_ffn_ln_g, L0_ffn_ln_b, L0_ffn_W1, L0_ffn_b1, L0_ffn_W2, L0_ffn_b2), axis=-1)
    return x

_drawn_inputs = setup_inputs


def setup_inputs(seed=0):
    import zlib

    import numpy as np

    out = dict(_drawn_inputs(seed))
    spreads = {'L0_attn_ln_w': (1.0, 0.589),
     'L0_attn_ln_b': (0.0, 0.1),
     'L0_ffn_ln_g': (1.0, 0.2),
     'L0_ffn_ln_b': (0.0, 0.1)}
    factors = {'L0_attn_time_maa_x': 5.283,
     'L0_attn_maa_w1': 3.086,
     'L0_attn_maa_w2': 3.589,
     'L0_attn_decay_w1': 6.897,
     'L0_attn_decay_w2': 8.0,
     'L0_attn_aaa_w1': 8.0,
     'L0_attn_aaa_w2': 8.0,
     'L0_attn_ma_w1': 8.0,
     'L0_attn_ma_w2': 8.0,
     'L0_attn_mk_w1': 8.0,
     'L0_attn_mk_w2': 8.0,
     'L0_attn_time_faaaa': 64.0,
     'L0_attn_time_aaaaa': 23.749,
     'L0_attn_time_misc_a': 41.672,
     'L0_attn_time_misc_k': 8.0,
     'L0_ffn_b1': 8.0,
     'L0_ffn_b2': 8.0}
    for name, (base, spread) in spreads.items():
        noise = np.random.default_rng([zlib.crc32(name.encode()), seed]).standard_normal(out[name].shape)
        drawn = base * np.exp(spread * noise) if base else spread * noise
        out[name] = jnp.asarray(drawn.astype(out[name].dtype))
    for name, factor in factors.items():
        out[name] = (out[name] * factor).astype(out[name].dtype)
    return out
```

```python
from contextlib import ExitStack

import concourse.bass as bass
from concourse import mybir

F32 = mybir.dt.float32
I32 = mybir.dt.int32
ALU = mybir.AluOpType
ACT = mybir.ActivationFunctionType
AX = mybir.AxisListType

P = 128
B, T, C = 8, 512, 256
HS = 16
H = C // HS
TB = 64
NBLK = T // TB
COLS = B * TB
SUB = 16
SLOTS = TB // SUB
HALF = C // P
GN_EPS = 0.00064
LN_EPS = 1e-05
DECAY = 0.6065306597126334
TINY = 1e-37
E, D, F = 8, C, 1024
FT = F // P
NTOK = B * T
NTILE = NTOK // P
EBLK = NTILE + E - 1
DEPTH = 3
assert EBLK % DEPTH == 0
CONSTS = {"slot": P, "eblock": EBLK, "prefer": E, "fill": NTILE, "row": NTILE}
PARAMS = ["maa_x", "maa0", "maa1", "maa2", "maa3", "decay", "aaaaa", "misc_a", "misc_k", "faaaa", "ln_w", "ln_b"]


class Steps:

    def __init__(self, sem, names):
        self.sem, self.names, self.seen = sem, names, 0

    def inc(self, name, ins):
        assert self.names[self.seen % len(self.names)] == name, (name, self.names[self.seen % len(self.names)])
        self.seen += 1
        return ins.then_inc(self.sem, 1)

    def value(self, blk, name):
        return blk * len(self.names) + self.names.index(name) + 1

    def wait(self, eng, blk, name):
        eng.wait_ge(self.sem, self.value(blk, name))


RING = 4
RING_JOBS = (["lo1"] + [f"lo2_{g}{h}" for g in range(4) for h in range(2)]
             + ["h1", "h2", "z0", "z1", "mk0", "mk1", "tg", "r0", "r1", "k0", "k1", "v0", "v1", "kk0", "kk1",
                "a0", "a1", "ma0", "ma1", "ss0", "ss1", "g0", "g1", "rk0", "rk1"])
POST_JOBS = ["yc0", "yc1", "var0", "var1", "wo0", "wo1", "xT0", "xT1", "logit"]


class Banks:

    def __init__(self, banks, jobs, filled, emptied_by):
        self.banks, self.jobs, self.filled, self.emptied_by = banks, jobs, filled, emptied_by

    def where(self, name):
        j = self.jobs.index(name)
        return j % len(self.banks), j

    def tile(self, name):
        return self.banks[self.where(name)[0]]

    def wait_empty(self, eng, blk, name, first):
        b, j = self.where(name)
        if j >= len(self.banks):
            steps, step = self.emptied_by[self.jobs[j - len(self.banks)]]
            steps.wait(eng, blk, step)
        elif not first:
            steps, step = self.emptied_by[self.jobs[b::len(self.banks)][-1]]
            steps.wait(eng, blk - 1, step)

    def fill(self, name, ins):
        return ins.then_inc(self.filled[self.where(name)[0]], 1)

    def wait_full(self, eng, blk, name):
        b, j = self.where(name)
        eng.wait_ge(self.filled[b], blk * len(self.jobs[b::len(self.banks)]) + j // len(self.banks) + 1)


class Waits:

    def __init__(self, eng, carrier):
        self.eng, self.carrier = eng, carrier

    def wait_ge(self, s, value):
        self.eng.wait_ge(s, value)
        if not isinstance(value, int):
            self.eng.sem_inc(self.carrier, 1)


def build(nc, d, out):
    with ExitStack() as ctx:
        sem = lambda name: ctx.enter_context(nc.semaphore(name))
        WORDS = 53208
        arena = ctx.enter_context(nc.sbuf_tensor("arena", [P, WORDS], F32))
        top = [0]

        def take(words):
            at = top[0]
            top[0] += words
            assert top[0] <= WORDS, top[0]
            return arena[:, at:at + words]

        def ct(ap=None):
            return (take(HALF * COLS) if ap is None else ap).rearrange("p (h n) -> p h n", h=HALF)

        def bt(ap):
            return ap.rearrange("p h (b t) -> p h b t", b=B)

        banks = [ctx.enter_context(nc.psum_tensor(f"bank{i}", [P, 512], F32)) for i in range(5)]
        ab_bank = [ctx.enter_context(nc.psum_tensor(f"ab{i}", [P, 512], F32)) for i in range(2)]
        ab = [b[:, :].rearrange("p (x t j) -> p x t j", x=2, t=SUB) for b in ab_bank]
        outer_bank = ctx.enter_context(nc.psum_tensor("outer", [P, 512], F32))
        outer = outer_bank[:, 0:HS * HS].rearrange("p (i j) -> p i j", i=HS)
        hid_ps = banks[0:2]
        hidT_ps = banks[2:4]
        xnT_ps = banks[4]
        y_ps = [ab_bank[0], ab_bank[1], outer_bank]
        route_ps = banks[0:3]

        w_sq = take(4 * HALF * C).rearrange("p (w k n) -> p w k n", w=4, k=HALF)
        w_maa1 = take(HALF * P).rearrange("p (k n) -> p k n", k=HALF)
        w_maa2 = take(C)
        w_gate1 = take(HALF * P).rearrange("p (k n) -> p k n", k=HALF)
        w_gate2 = take(C)
        w_h1 = take(HALF * 96).rearrange("p (k n) -> p k n", k=HALF)
        w_h2 = take(HALF * 64).rearrange("p (k n) -> p k n", k=HALF)
        w_out1 = take(3 * C)[0:96, :].rearrange("p (w n) -> p w n", w=3)
        w_out2 = take(2 * C)[0:64, :].rearrange("p (w n) -> p w n", w=2)
        mats = take(4 * P).rearrange("p (m n) -> p m n", m=4)
        head_sum, head_mean, centre, ident = (mats[:, i, :] for i in range(4))
        cent = take(HALF * 8).rearrange("p (k e) -> p k e", k=HALF)
        par = take(len(PARAMS) * HALF).rearrange("p (w h) -> p w h", h=HALF)
        negp = take(HALF)
        tiny = take(1)
        gneps = take(1)
        lneps = take(1)
        spare = take(1)
        ones = take(TB)
        logits = take(NTILE * 8).rearrange("p (n e) -> p n e", e=8)

        def prm(name, h):
            i = PARAMS.index(name)
            return par[:, i, h:h + 1]

        at_proj = top[0]
        xT = take(HALF * B * (TB + 1)).rearrange("p (h b t) -> p h b t", h=HALF, b=B)
        x_now, x_prev = xT[:, :, :, 1:TB + 1], xT[:, :, :, 0:TB]
        dx = ct()
        zt = dx
        xm = [ct() for _ in range(4)]
        mix = xm[3]
        L, iW, rkt = xm[0], xm[1], xm[2]
        lo1 = take(COLS)
        h1 = lo1
        h2 = take(COLS)
        tg = take(COLS)
        ao_flat = take(HALF * B * (TB + 1))
        ao = ao_flat.rearrange("p (h b t) -> p h b t", h=HALF, b=B)
        nrm = ct(ao_flat[:, 0:HALF * COLS])
        kk, rt, kt, vt, at, ma, nma, mk, t1 = (ct() for _ in range(9))
        Wt = take(HALF * B * (TB + 1)).rearrange("p (h b t) -> p h b t", h=HALF, b=B)
        gt, gp, ut, up = (ct() for _ in range(4))
        at_rec = top[0]
        PA = take(HS * (TB + 1)).rearrange("p (c t) -> p c t", c=HS)
        PX = take(4 * HS * TB).rearrange("p (x c t) -> p x c t", x=4, c=HS)
        kqv = take(2 * 3 * SUB * HS).rearrange("p (s x t c) -> p s x t c", s=2, x=3, t=SUB)
        Sh = take(2 * SUB * HS * HS).rearrange("p (s t i j) -> p s t i j", s=2, t=SUB, i=HS)
        VK = take(8 * HS * HS).rearrange("p (t i j) -> p t i j", t=8, i=HS)
        S0 = take(HS * HS).rearrange("p (i j) -> p i j", i=HS)
        Z = take(2 * HS * HS).rearrange("p (t i j) -> p t i j", t=2, i=HS)
        M = take(HS * HS).rearrange("p (i j) -> p i j", i=HS)
        SA = take(HS)
        Wend = take(HS)
        ysb = take(HS * TB).rearrange("p (i t) -> p i t", i=HS)
        at_yc = top[0]
        yc = ct()
        ysq = ct()
        x1T = ct(ysq.rearrange("p h n -> p (h n)"))
        at_xtok = top[0]
        xtok = take(4 * C).rearrange("p (j c) -> p j c", j=4)
        stats = take(4 * 6).rearrange("p (j c) -> p j c", j=4)
        mv = take(4 * 2).rearrange("p (j c) -> p j c", j=4)
        rstd = take(4)
        def view(at, words):
            return arena[:, at:at + words]

        W1 = view(at_proj, E * HALF * F).rearrange("p (e k f) -> p e k f", e=E, k=HALF)
        at_rows = at_proj + E * HALF * F
        assert at_rows + 3 * E * D <= at_rec
        rows = view(at_rows, 3 * E * D).rearrange("p (w e n) -> p w e n", w=3, e=E)
        W2 = view(at_rec, E * FT * D).rearrange("p (e t n) -> p e t n", e=E, t=FT)
        hid = view(at_yc, F)
        hidT = view(at_yc + F, F).rearrange("p (t n) -> p t n", t=FT)
        xn = view(at_xtok, D)
        xnT = view(at_xtok + D, D).rearrange("p (k n) -> p k n", k=HALF)
        b1 = take(E * FT).rearrange("p (e t) -> p e t", e=E)
        table = take(EBLK).bitcast(I32)
        expert = take(EBLK).bitcast(I32)
        gidx = take(DEPTH).bitcast(I32)
        sidx = take(DEPTH).bitcast(I32)
        estat = take(2 * 6).rearrange("p (w s) -> p w s", w=2)
        emv = take(2 * 2).rearrange("p (w s) -> p w s", w=2)
        erstd = take(2)
        at_blk = top[0]
        xg = take(DEPTH * D).rearrange("p (s n) -> p s n", s=DEPTH)
        zb = take(DEPTH * D).rearrange("p (s n) -> p s n", s=DEPTH)
        ob = take(DEPTH * D).rearrange("p (s n) -> p s n", s=DEPTH)
        at_cst = 0
        tri = view(0, P)
        all_ones = view(P, P)
        cst, at_c = {}, 2 * P
        for n, w in CONSTS.items():
            cst[n] = view(at_c, w)
            at_c += w
        assert at_c <= 3 * HALF * C
        at_tmp = [at_blk]

        def tmp(words):
            v = view(at_tmp[0], words)
            at_tmp[0] += words
            assert at_tmp[0] <= top[0]
            return v

        ne = lambda ap: ap.rearrange("p (n e) -> p n e", e=E)
        onehot = ne(tmp(NTILE * E))
        place = ne(tmp(NTILE * E))
        run = tmp(NTILE * E).rearrange("p (e n) -> p e n", e=E)
        cmp = tmp(EBLK * E)
        best = tmp(NTILE)
        blocks = tmp(E)
        blk_end = tmp(E)
        posf, slotf, blkf = tmp(NTILE), tmp(NTILE), tmp(NTILE)
        posi, slotp, blki = tmp(NTILE).bitcast(I32), tmp(NTILE).bitcast(I32), tmp(NTILE).bitcast(I32)
        RSEL = 4
        in_slot = tmp(RSEL * P).rearrange("p (s n) -> p s n", s=RSEL)
        in_blk = tmp(RSEL * EBLK).rearrange("p (s n) -> p s n", s=RSEL)
        efl = tmp(EBLK)

        xd_a = nc.dram_tensor("scr_a", (B, C, TB + 1), F32, kind="Internal").ap()
        xd_x = nc.dram_tensor("scr_x", (4, B, C, TB), F32, kind="Internal").ap()
        yd = nc.dram_tensor("scr_y", (B, C, TB), F32, kind="Internal").ap()
        x1d = nc.dram_tensor("scr_x1", (B, T, C), F32, kind="Internal").ap()

        w_in = sem("weights_in")
        carrier = sem("wait_carrier")
        carrier_pool = sem("wait_carrier_pool")
        const_ok = sem("const_ok")
        xT_in = sem("xT_in")
        mixed = Steps(sem("mixed"), ["dx", "mix0", "mix1"])
        xm_ok = Steps(sem("xm_ok"), [f"{g}{h}" for g in range(4) for h in range(2)])
        lo_ok = Steps(sem("lo_ok"), ["lo1"])
        proj = Steps(sem("proj"), ["h1t", "h1c", "h2t", "h2c", "z0", "abs0", "sg0", "z1", "abs1", "sg1", "mk0", "mk1", "exp", "ln",
                                   "tg", "r0", "r1", "k0", "k1", "v0", "v1", "kk0", "sq0", "kk1", "sq1",
                                   "a0", "a1", "ma0", "nma0", "ma1", "nma1", "lnss0", "lnss1", "inv"])
        comb_act = Steps(sem("comb_act"), ["W", "iW", "ek", "g0", "g1"])
        comb = Steps(sem("comb"), ["ls", "e2"] + [f"scan{i}" for i in range(HALF * B)]
                     + ["kkn", "t", "f", "k2", "bt", "k3", "rk0", "rk1", "ao", "aend", "q", "b", "k", "u0", "u1"])
        handed = Steps(sem("handed"), ["gp", "up"])
        scr_out = sem("scr_out")
        pair_in = sem("pair_in")
        relayed = sem("relayed")
        s0_ok = sem("s0_ok")
        s_ok = sem("s_ok")
        chain = sem("chain")
        vk_ok = sem("vk_ok")
        z_ok = sem("z_ok")
        qm_ok = sem("qm_ok")
        yr_ok = sem("yr_ok")
        y_out = sem("y_out")
        y_in = sem("y_in")
        post_act = Steps(sem("post_act"), ["c0", "s0", "c1", "s1", "ln0", "ln1", "rstd", "x1T0", "x1T1"])
        post_dve = Steps(sem("post_dve"), ["n", "w0", "w1", "g0", "g1"])
        tok = Steps(sem("tok"), [f"z{j}" for j in range(4)] + [f"st{j}" for j in range(4)] + ["settle"]
                    + [f"ag{j}" for j in range(4)]
                    + [f"x1_{j}" for j in range(4)] + ["lg"])
        rst = Steps(sem("rst"), ["ln", "exp"])
        freed = {"lo1": (lo_ok, "lo1"), "h1": (proj, "h1c"), "h2": (proj, "h2c"), "tg": (proj, "tg")}
        for h in "01":
            freed.update({f"lo2_{g}{h}": (xm_ok, f"{g}{h}") for g in range(4)})
            freed.update({f"{n}{h}": (proj, f"{n}{h}") for n in ("r", "k", "v", "a", "mk")})
            freed.update({f"kk{h}": (proj, f"sq{h}"), f"ma{h}": (proj, f"nma{h}"), f"z{h}": (proj, f"sg{h}"),
                          f"ss{h}": (proj, f"lnss{h}"), f"g{h}": (comb_act, f"g{h}"), f"rk{h}": (comb, f"u{h}")})
        ring = Banks(banks[:RING], RING_JOBS, [sem(f"filled{i}") for i in range(RING)], freed)
        freed = {"wo0": (tok, "z1"), "wo1": (tok, "z3"), "logit": (tok, "lg")}
        for h in "01":
            freed.update({f"yc{h}": (post_act, f"s{h}"), f"var{h}": (post_act, f"ln{h}"), f"xT{h}": (post_act, f"x1T{h}")})
        post = Banks(banks[RING:], POST_JOBS, [sem("post_filled")], freed)
        xtok_in = sem("xtok_in")
        x1_out = sem("x1_out")

        route_in = sem("route_in")
        route = Steps(sem("route"), ["max", "eq", "code", "cmax", "onehot", "sum"] + [f"run{e}" for e in range(E)]
                      + ["cnt", "nblk", "bend", "bstart", "excl", "p1", "p2", "p3", "pos", "posi", "slot", "blk", "slotf", "blkf",
                         "ecmp", "esum", "expert"])
        route_pe = Steps(sem("route_pe"), ["rank", "table"])
        sel_ok = sem("sel_ok")
        sel_used = sem("sel_used")
        table_ok = sem("table_ok")
        w1_in = [sem(f"w1_in{e}") for e in range(E)]
        w2_in = [sem(f"w2_in{e}") for e in range(E)]
        rows_in = sem("rows_in")
        xg_clear = sem("xg_clear")
        w1_ready = sem("w1_ready")
        w2_ready = sem("w2_ready")
        gathered = [sem(f"gathered{i}") for i in range(DEPTH)]
        idx_ok = Steps(sem("idx_ok"), ["gather"])
        sidx_ok = Steps(sem("sidx_ok"), ["scatter"])
        scattered = [sem(f"scattered{i}") for i in range(DEPTH)]
        prep = Steps(sem("prep"), ["st", "settle", "ag", "xh", "g", "l", "zb"])
        prep_act = Steps(sem("prep_act"), ["ln", "exp"])
        xnT_ok = Steps(sem("xnT_ok"), ["x"])
        hid_ok = Steps(sem("hid_ok"), ["0", "1"])
        relu_act = Steps(sem("relu_act"), [str(t) for t in range(FT // 2)])
        relu_dve = Steps(sem("relu_dve"), [str(t) for t in range(FT // 2, FT)])
        fin = Steps(sem("fin"), ["z", "st", "settle", "ag", "o"])
        fin_act = Steps(sem("fin_act"), ["ln", "exp"])
        turned_x = Steps(sem("turned_x"), ["x"])
        turned_h = Steps(sem("turned_h"), ["h"])
        first_mm = Steps(sem("first_mm"), ["0", "1"])
        second_mm = Steps(sem("second_mm"), ["y"])

        block = ctx.enter_context(nc.Block())
        last = NBLK - 1

        @block.sync
        def _(sp):
            w = Waits(sp, carrier)

            loads = [(w_sq[:, i], d[n].rearrange("(k p) n -> p k n", p=P)) for i, n in enumerate(["WrT", "WkT", "WvT", "WoT"])]
            loads += [(w_maa1, d["maa1T"].rearrange("(k p) n -> p k n", p=P)), (w_maa2, d["maa2"]),
                      (w_gate1, d["gate1T"].rearrange("(k p) n -> p k n", p=P)), (w_gate2, d["gate2"]),
                      (w_h1, d["h1T"].rearrange("(k p) n -> p k n", p=P)), (w_h2, d["h2T"].rearrange("(k p) n -> p k n", p=P)),
                      (w_out1, d["out1"].rearrange("w p n -> p w n")), (w_out2, d["out2"].rearrange("w p n -> p w n")),
                      (mats, d["mats"].rearrange("m p n -> p m n")), (cent, d["centT"].rearrange("(k p) e -> p k e", p=P)),
                      (par, d["par"])]

            def load_xT(m):
                for h in range(HALF):
                    sp.dma_start(xT[:, h], d["xTp"][h * P:(h + 1) * P, :, bass.ds(m * TB, TB + 1)]).then_inc(xT_in, 16)

            load_xT(0)
            for dst, src in loads:
                sp.dma_start(dst, src).then_inc(w_in, 16)
            assert len(loads) == d["_nloads"]

            def next_xT(m):
                ring.wait_full(w, m - 1, "v1")
                ring.wait_full(w, m - 1, "kk0")
                ring.wait_full(w, m - 1, "kk1")
                mixed.wait(w, m - 1, "mix1")
                load_xT(m)

            def y_turn(m):
                w.wait_ge(yr_ok, (m * SLOTS + SLOTS) * 4)
                sp.dma_start(yd.rearrange("b (h i) t -> (b h) (i t)", h=H), ysb.rearrange("p i t -> p (i t)")).then_inc(y_out, 16)
                w.wait_ge(y_out, (m + 1) * 16)
                if not (isinstance(m, int) and m == 0):
                    post_wait_prev(sp, m)
                for h in range(HALF):
                    sp.dma_start(bt(yc)[:, h], yd[:, h * P:(h + 1) * P, :].rearrange("b p t -> p b t")).then_inc(y_in, 16)
                for e in range(2):
                    sp.dma_start(xtok[e * 64:(e + 1) * 64, :, :],
                                 d["x"][:, bass.ds(m * TB, TB), :].rearrange("(j e) t c -> e t j c", e=2)[e]
                                 ).then_inc(xtok_in, 16)

            def post_wait_prev(sp, m):
                post.wait_full(w, m - 1, "wo1")
                w.wait_ge(x1_out, m * 32)
                post.wait_full(w, m - 1, "xT1")

            def to_pairs(m):
                if not (isinstance(m, int) and m == 0):
                    w.wait_ge(pair_in, m * 80)
                for i, (src, step) in enumerate([(vt, None), (ao, "aend"), (rt, "q"), (at, "b"), (kt, "k")]):
                    if step is None:
                        proj.wait(w, m, "v1")
                    else:
                        comb.wait(w, m, step)
                    x = {0: 2, 2: 1, 3: 3, 4: 0}.get(i)
                    for h in range(HALF):
                        if x is None:
                            sp.dma_start(xd_a[:, h * P:(h + 1) * P, :].rearrange("b p t -> p b t"), ao[:, h]).then_inc(scr_out, 16)
                        else:
                            sp.dma_start(xd_x[x, :, h * P:(h + 1) * P, :].rearrange("b p t -> p b t"), bt(src)[:, h]).then_inc(scr_out, 16)
                w.wait_ge(scr_out, (m + 1) * 160)
                if not (isinstance(m, int) and m == 0):
                    w.wait_ge(relayed, m * SLOTS * 2)
                sp.dma_start(PA.rearrange("p c t -> p (c t)"), xd_a.rearrange("b (h c) t -> (b h) (c t)", h=H)).then_inc(pair_in, 16)
                for x in range(4):
                    sp.dma_start(PX[:, x].rearrange("p c t -> p (c t)"),
                                 xd_x[x].rearrange("b (h c) t -> (b h) (c t)", h=H)).then_inc(pair_in, 16)

            def store_x1(m):
                tok.wait(w, m, "x1_3")
                for e in range(2):
                    sp.dma_start(x1d[:, bass.ds(m * TB, TB), :].rearrange("(j e) t c -> e t j c", e=2)[e],
                                 xtok[e * 64:(e + 1) * 64, :, :]).then_inc(x1_out, 16)

            next_xT(1)
            to_pairs(0)

            def body(n, first, ahead):
                if not first:
                    y_turn(n - 1)
                if ahead == 2:
                    next_xT(n + 2)
                if ahead:
                    to_pairs(n + 1)
                if not first:
                    store_x1(n - 1)

            body(0, True, 2)
            body(1, False, 2)
            with sp.Fori(2, last - 1) as n:
                body(n, False, 2)
            body(last - 1, False, 1)
            to_pairs_over = NBLK * 80
            w.wait_ge(pair_in, to_pairs_over)
            comb.wait(w, last, "u1")
            sp.dma_start(view(0, 2 * P).rearrange("p (m n) -> p m n", m=2), d["mats2"].rearrange("m p n -> p m n")).then_inc(route_in, 16)
            sp.dma_start(view(2 * P, sum(CONSTS.values())), d["cst"]).then_inc(route_in, 16)
            sp.dma_start(b1.rearrange("p e t -> p (e t)"), d["b1T"]).then_inc(route_in, 16)
            for e in range(E):
                sp.dma_start(W1[:, e], d["W1"][e].rearrange("(k p) f -> p k f", p=P)).then_inc(w1_in[e], 16)
            body(last, False, 0)
            y_turn(last)
            w.wait_ge(s_ok, NBLK * SLOTS * 32)
            w.wait_ge(yr_ok, NBLK * SLOTS * 4)
            for e in range(E):
                sp.dma_start(W2[:, e], d["W2"][e].rearrange("(t p) n -> p t n", p=P)).then_inc(w2_in[e], 16)
            post_dve.wait(w, last, "g1")
            for i, n in enumerate(("ln_g", "ln_b", "b2")):
                sp.dma_start(rows[:, i].rearrange("p e n -> p (e n)"), d[n].partition_broadcast(P)).then_inc(rows_in, 16)
            store_x1(last)
            w.wait_ge(rows_in, 48)
            for e in range(E):
                w.wait_ge(w1_in[e], 16)
                sp.sem_inc(w1_ready, 1)
            for e in range(E):
                w.wait_ge(w2_in[e], 16)
                sp.sem_inc(w2_ready, 1)

        @block.tensor
        def _(pe):
            def job(bk, m, name, first, parts, rows=P, cols=COLS):
                bk.wait_empty(pe, m, name, first)
                out_ap = bk.tile(name)[0:rows, 0:cols]
                for i, (lhsT, rhs) in enumerate(parts):
                    mm = pe.matmul(out_ap, lhsT, rhs, start=(i == 0), stop=(i == len(parts) - 1))
                bk.fill(name, mm)

            def both(m, name, w, g, extra=(), cols=None, rows=P):
                first = isinstance(m, int) and m == 0
                sl = cols
                parts = [(w[:, k, sl], x_now[:, k]) for k in range(HALF)]
                parts += [(w[:, k, sl], bt(xm[g])[:, k]) for k in range(HALF)]
                parts += list(extra)
                ring.wait_empty(pe, m, name, first)
                o = ring.tile(name)[0:rows, :]
                for i, (lhsT, rhs) in enumerate(parts):
                    mm = pe.matmul(o.rearrange("p (b t) -> p b t", b=B), lhsT, rhs, start=(i == 0), stop=(i == len(parts) - 1))
                ring.fill(name, mm)

            def low(m):
                first = isinstance(m, int) and m == 0
                mixed.wait(pe, m, "mix1")
                job(ring, m, "lo1", first, [(w_maa1[:, k, :], mix[:, k]) for k in range(HALF)])
                lo_ok.wait(pe, m, "lo1")
                for g in range(4):
                    for h in range(HALF):
                        job(ring, m, f"lo2_{g}{h}", first,
                            [(w_maa2[32 * g:32 * g + 32, h * P:(h + 1) * P], lo1[32 * g:32 * g + 32, :])])

            def project(m):
                first = False
                hs = lambda h: slice(h * P, (h + 1) * P)
                xm_ok.wait(pe, m, "11")
                both(m, "h1", w_h1, 1, cols=slice(0, 96), rows=96)
                xm_ok.wait(pe, m, "21")
                both(m, "h2", w_h2, 2, cols=slice(0, 64), rows=64)
                proj.wait(pe, m, "h1c")
                for h in range(HALF):
                    job(ring, m, f"z{h}", first, [(w_out1[:, 0, hs(h)], h1[0:96, :])])
                proj.wait(pe, m, "h2c")
                for h in range(HALF):
                    job(ring, m, f"mk{h}", first, [(w_out2[:, 1, hs(h)], h2[0:64, :])])
                both(m, "tg", w_gate1, 0, cols=slice(0, P))
                for h in range(HALF):
                    both(m, f"r{h}", w_sq[:, 0], 0, cols=hs(h))
                for h in range(HALF):
                    both(m, f"k{h}", w_sq[:, 1], 2, cols=hs(h))
                xm_ok.wait(pe, m, "31")
                for h in range(HALF):
                    both(m, f"v{h}", w_sq[:, 2], 3, cols=hs(h))
                h2v = h2[0:64, :].rearrange("p (b t) -> p b t", b=B)
                for h in range(HALF):
                    both(m, f"kk{h}", w_sq[:, 1], 2, cols=hs(h), extra=[(w_out2[:, 0, hs(h)], h2v)])
                for h in range(HALF):
                    job(ring, m, f"a{h}", first, [(w_out1[:, 1, hs(h)], h1[0:96, :])])
                for h in range(HALF):
                    job(ring, m, f"ma{h}", first, [(w_out1[:, 2, hs(h)], h1[0:96, :])])
                proj.wait(pe, m, "sq1")
                for h in range(HALF):
                    job(ring, m, f"ss{h}", first, [(head_sum, nrm[:, h])])

            def gates(m):
                proj.wait(pe, m, "tg")
                for h in range(HALF):
                    job(ring, m, f"g{h}", False, [(w_gate2[:, h * P:(h + 1) * P], tg)])
                comb.wait(pe, m, "rk1")
                for h in range(HALF):
                    job(ring, m, f"rk{h}", False, [(head_sum, rkt[:, h])])

            def norm(m):
                first = isinstance(m, int) and m == 0
                pe.wait_ge(y_in, (m + 1) * 32)
                for h in range(HALF):
                    job(post, m, f"yc{h}", first, [(centre, yc[:, h])])
                for h in range(HALF):
                    post_act.wait(pe, m, f"s{h}")
                    job(post, m, f"var{h}", first, [(head_mean, ysq[:, h])])

            def project_out(m):
                first = isinstance(m, int) and m == 0
                for w in range(2):
                    post.wait_empty(pe, m, f"wo{w}", first)
                    post_dve.wait(pe, m, "g1")
                    for j in (2 * w, 2 * w + 1):
                        for h in range(HALF):
                            mm = pe.matmul(post.tile("wo0")[:, (j % 2) * C:(j % 2 + 1) * C], yc[:, h, j * P:(j + 1) * P],
                                           w_sq[:, 3, h, :], start=(h == 0), stop=(h == HALF - 1))
                    post.fill(f"wo{w}", mm)

            def router(m):
                first = isinstance(m, int) and m == 0
                for w in range(2):
                    post.wait_empty(pe, m, f"xT{w}", first)
                    tok.wait(pe, m, "x1_3")
                    for q in range(4):
                        j, h = 2 * w + q // 2, q % 2
                        mm = pe.transpose(post.tile("xT0")[:, q * P:(q + 1) * P], xtok[:, j, h * P:(h + 1) * P], ident)
                    post.fill(f"xT{w}", mm)
                post.wait_empty(pe, m, "logit", first)
                post_act.wait(pe, m, "x1T1")
                x1q = x1T.rearrange("p h n -> p (h n)")
                for j in range(4):
                    for h in range(HALF):
                        mm = pe.matmul(post.tile("logit")[:, 8 * j:8 * j + 8], x1q[:, (2 * j + h) * P:(2 * j + h + 1) * P],
                                       cent[:, h, :], start=(h == 0), stop=(h == HALF - 1))
                post.fill("logit", mm)

            pe.wait_ge(w_in, 16 * d["_nloads"])
            low(0)
            project(0)
            gates(0)
            low(1)

            def body(n, first, ahead):
                if ahead:
                    project(n + 1)
                if not first:
                    norm(n - 1)
                if ahead:
                    gates(n + 1)
                if not first:
                    project_out(n - 1)
                    router(n - 1)
                if ahead == 2:
                    low(n + 2)

            body(0, True, 2)
            body(1, False, 2)
            with pe.Fori(2, last - 1) as n:
                body(n, False, 2)
            body(last - 1, False, 1)
            body(last, False, 0)
            norm(last)
            project_out(last)
            router(last)

            pe.wait_ge(route_in, 48)
            route.wait(pe, 0, "onehot")
            oh = onehot.rearrange("p n e -> p (n e)")
            pe.matmul(route_ps[0][:, 0:NTILE * E], tri, oh, start=True, stop=True)
            route_pe.inc("rank", pe.matmul(route_ps[1][:, 0:NTILE * E], all_ones, oh, start=True, stop=True))
            for n in range(NTILE):
                pe.wait_ge(sel_ok, n + 1)
                mm = pe.matmul(route_ps[2][:, 0:EBLK], in_slot[:, n % RSEL], in_blk[:, n % RSEL],
                               start=(n == 0), stop=(n == NTILE - 1))
                if n < NTILE - 1:
                    mm.then_inc(sel_used, 1)
            route_pe.inc("table", mm)

            def turn_x(j, s):
                prep.wait(pe, j, "l")
                if not (isinstance(j, int) and j == 0):
                    xnT_ok.wait(pe, j - 1, "x")
                for k in range(HALF):
                    mm = pe.transpose(xnT_ps[:, k * P:(k + 1) * P], xn[:, k * P:(k + 1) * P], ident)
                turned_x.inc("x", mm)

            def expert_of(j):
                return pe.value_load(expert[0:1, bass.ds(j, 1)], min_val=0, max_val=E - 1)

            def first_layer(j):
                e = expert_of(j)
                xnT_ok.wait(pe, j, "x")
                if not (isinstance(j, int) and j == 0):
                    hid_ok.wait(pe, j - 1, "1")
                pe.wait_ge(w1_ready, e + 1)
                for i in range(2):
                    for k in range(HALF):
                        mm = pe.matmul(hid_ps[i][:, :], xnT[:, k, :],
                                       W1f[:, bass.ds(e * (HALF * F) + k * F + i * 512, 512)],
                                       start=(k == 0), stop=(k == HALF - 1))
                    first_mm.inc(str(i), mm)

            def turn_h(j):
                if not (isinstance(j, int) and j == 0):
                    relu_act.wait(pe, j - 1, str(FT // 2 - 1))
                    relu_dve.wait(pe, j - 1, str(FT - 1))
                hid_ok.wait(pe, j, "1")
                for t in range(FT):
                    mm = pe.transpose(hidT_ps[t // 4][:, (t % 4) * P:(t % 4 + 1) * P], hid[:, t * P:(t + 1) * P], ident)
                turned_h.inc("h", mm)

            def second_layer(j, s):
                e = expert_of(j)
                relu_act.wait(pe, j, str(FT // 2 - 1))
                relu_dve.wait(pe, j, str(FT - 1))
                if not (isinstance(j, int) and j < DEPTH):
                    fin.wait(pe, j - DEPTH, "z")
                pe.wait_ge(w2_ready, e + 1)
                for t in range(FT):
                    mm = pe.matmul(y_ps[s][:, 0:D], hidT[:, t, :], W2f[:, bass.ds(e * (FT * D) + t * D, D)],
                                   start=(t == 0), stop=(t == FT - 1))
                second_mm.inc("y", mm)

            W1f = view(at_proj, E * HALF * F)
            W2f = view(at_rec, E * FT * D)
            turn_x(0, 0)
            first_layer(0)
            turn_x(1, 1)

            def iteration(j, s):
                turn_h(j)
                if not (isinstance(j, int) and j + 1 >= EBLK):
                    first_layer(j + 1)
                if not (isinstance(j, int) and j + 2 >= EBLK):
                    turn_x(j + 2, (s + 2) % DEPTH)
                second_layer(j, s)

            for s in range(DEPTH):
                iteration(s, s)
            with pe.Fori(1, EBLK // DEPTH - 1) as i:
                for s in range(DEPTH):
                    iteration(i * DEPTH + s, s)
            for s in range(DEPTH):
                iteration(EBLK - DEPTH + s, s)

        @block.scalar
        def _(act):
            A = nc.scalar.activation

            def relay(q_blk, s):
                q = q_blk * SLOTS + s
                if s == 0:
                    act.wait_ge(pair_in, (q_blk + 1) * 80)
                p = s % 2
                zero = isinstance(q_blk, int) and q_blk == 0
                if not (zero and s < 2):
                    act.wait_ge(s_ok, (q - 1) * 32)
                    act.wait_ge(qm_ok, (q - 1) * 4)
                t = slice(s * SUB, (s + 1) * SUB)
                if s == SLOTS - 1:
                    A(Wend, PA[:, :, TB], ACT.Copy)
                A(ab[p][:, 0], PA[:, :, t].rearrange("p c t -> p t c"), ACT.Copy)
                A(ab[p][:, 1], PX[:, 3, :, t].rearrange("p c t -> p t c"), ACT.Copy).then_inc(relayed, 1)
                A(kqv[:, p], PX[:, 0:3, :, t].rearrange("p x c t -> p x t c"), ACT.Copy).then_inc(relayed, 1)

            def low(m):
                ring.wait_full(act, m, "lo1")
                if not (isinstance(m, int) and m == 0):
                    ring.wait_full(act, m - 1, "ma1")
                lo_ok.inc("lo1", A(lo1, ring.tile("lo1")[:, :], ACT.Tanh))

            def evac(m):
                first = isinstance(m, int) and m == 0

                def ev(step, name, dst, func, rows=slice(0, P), **kw):
                    ins = A(dst, ring.tile(name)[rows, :], func, **kw)
                    proj.inc(step, ins)

                ring.wait_full(act, m, "h1")
                ev("h1t", "h1", h1[0:64, :], ACT.Tanh, slice(0, 64))
                ev("h1c", "h1", h1[64:96, :], ACT.Copy, slice(64, 96))
                ring.wait_full(act, m, "h2")
                ev("h2t", "h2", h2[0:32, :], ACT.Tanh, slice(0, 32))
                ev("h2c", "h2", h2[32:64, :], ACT.Copy, slice(32, 64))
                for h in range(HALF):
                    ring.wait_full(act, m, f"z{h}")
                    ev(f"z{h}", f"z{h}", zt[:, h], ACT.Identity, bias=prm("decay", h))
                    ev(f"abs{h}", f"z{h}", t1[:, h], ACT.Abs, bias=prm("decay", h))
                    proj.inc(f"sg{h}", A(Wt[:, h, :, 1:TB + 1], bt(ring.tile(f"z{h}")[:, None, :])[:, 0], ACT.Sigmoid,
                                         bias=prm("decay", h)))
                for h in range(HALF):
                    ring.wait_full(act, m, f"mk{h}")
                    ev(f"mk{h}", f"mk{h}", mk[:, h], ACT.Sigmoid, bias=prm("misc_k", h))
                proj.wait(act, m, "abs1")
                proj.inc("exp", A(t1, t1, ACT.Exp, scale=-1.0))
                proj.wait(act, m, "exp")
                proj.inc("ln", A(t1, t1, ACT.Ln, bias=1.0))
                if not first:
                    ring.wait_full(act, m - 1, "g1")
                ring.wait_full(act, m, "tg")
                ev("tg", "tg", tg, ACT.Tanh)
                if not first:
                    act.wait_ge(scr_out, m * 160)
                    comb.wait(act, m - 1, "u1")
                for nm, dst in (("r", rt), ("k", kt), ("v", vt)):
                    for h in range(HALF):
                        ring.wait_full(act, m, f"{nm}{h}")
                        ev(f"{nm}{h}", f"{nm}{h}", dst[:, h], ACT.Copy)
                for h in range(HALF):
                    ring.wait_full(act, m, f"kk{h}")
                    ev(f"kk{h}", f"kk{h}", kk[:, h], ACT.Copy)
                    ev(f"sq{h}", f"kk{h}", nrm[:, h], ACT.Square)
                for h in range(HALF):
                    ring.wait_full(act, m, f"a{h}")
                    ev(f"a{h}", f"a{h}", at[:, h], ACT.Sigmoid, bias=prm("aaaaa", h))
                for h in range(HALF):
                    ring.wait_full(act, m, f"ma{h}")
                    ev(f"ma{h}", f"ma{h}", ma[:, h], ACT.Sigmoid, bias=prm("misc_a", h))
                    ev(f"nma{h}", f"ma{h}", nma[:, h], ACT.Sigmoid, bias=negp[:, h:h + 1], scale=-1.0)
                for h in range(HALF):
                    ring.wait_full(act, m, f"ss{h}")
                    ev(f"lnss{h}", f"ss{h}", nrm[:, h], ACT.Ln, bias=tiny)
                proj.wait(act, m, "lnss1")
                proj.inc("inv", A(nrm, nrm, ACT.Exp, scale=-0.5))

            def norm_act(m):
                for h in range(HALF):
                    post.wait_full(act, m, f"yc{h}")
                    post_act.inc(f"c{h}", A(yc[:, h], post.tile("yc0")[:, :], ACT.Copy))
                    ins = A(ysq[:, h], post.tile("yc0")[:, :], ACT.Square)
                    post_act.inc(f"s{h}", ins)
                for h in range(HALF):
                    post.wait_full(act, m, f"var{h}")
                    ins = A(ysq[:, h], post.tile("var0")[:, :], ACT.Ln, bias=gneps)
                    post_act.inc(f"ln{h}", ins)
                post_act.wait(act, m, "ln1")
                post_act.inc("rstd", A(ysq, ysq, ACT.Exp, scale=-0.5))

            def hand_over(m, first):
                if not first:
                    post_dve.wait(act, m - 1, "g1")
                comb_act.wait(act, m, "g1")
                handed.inc("gp", A(gp, gt, ACT.Copy))
                comb.wait(act, m, "u1")
                handed.inc("up", A(up, ut, ACT.Copy))

            def combine_act(m):
                comb.wait(act, m, f"scan{HALF * B - 1}")
                comb_act.inc("W", A(Wt[:, :, :, 1:TB + 1], bt(L), ACT.Exp, scale=-DECAY))
                comb_act.inc("iW", A(iW, L, ACT.Exp, scale=DECAY))
                comb.wait(act, m, "e2")
                comb_act.inc("ek", A(mk, mk, ACT.Exp))

            def gate_act(m):
                if not (isinstance(m, int) and m == 0):
                    handed.wait(act, m - 1, "gp")
                for h in range(HALF):
                    ring.wait_full(act, m, f"g{h}")
                    ins = A(gt[:, h], ring.tile(f"g{h}")[:, :], ACT.Copy)
                    comb_act.inc(f"g{h}", ins)

            def tok_rstd(m):
                tok.wait(act, m, "ag3")
                rst.inc("ln", A(rstd, mv[:, :, 1], ACT.Ln, bias=lneps))
                rst.wait(act, m, "ln")
                rst.inc("exp", A(rstd, rstd, ACT.Exp, scale=-0.5))

            def x1T_act(m):
                for w in range(2):
                    post.wait_full(act, m, f"xT{w}")
                    ins = A(x1T[:, w], post.tile("xT0")[:, :], ACT.Copy)
                    post_act.inc(f"x1T{w}", ins)

            act.wait_ge(w_in, 16 * d["_nloads"])
            act.wait_ge(const_ok, 6)
            low(0)
            evac(0)
            combine_act(0)
            gate_act(0)
            low(1)
            relay(0, 0)

            def body(n, first, ahead):
                relay(n, 1)
                if ahead:
                    evac(n + 1)
                relay(n, 2)
                if ahead:
                    combine_act(n + 1)
                if not first:
                    norm_act(n - 1)
                relay(n, 3)
                hand_over(n, first)
                if ahead:
                    gate_act(n + 1)
                if not first:
                    tok_rstd(n - 1)
                    x1T_act(n - 1)
                if ahead == 2:
                    low(n + 2)
                if ahead:
                    relay(n + 1, 0)

            body(0, True, 2)
            with act.Fori(1, last - 1) as n:
                body(n, False, 2)
            body(last - 1, False, 1)
            body(last, False, 0)
            norm_act(last)
            tok_rstd(last)
            x1T_act(last)

            def expert_of(j):
                return act.value_load(expert[0:1, bass.ds(j, 1)], min_val=0, max_val=E - 1)

            def root(steps, dve_steps, j, w):
                dve_steps.wait(act, j, "ag")
                steps.inc("ln", A(erstd[:, w:w + 1], emv[:, w, 1:2], ACT.Ln, bias=lneps))
                steps.wait(act, j, "ln")
                steps.inc("exp", A(erstd[:, w:w + 1], erstd[:, w:w + 1], ACT.Exp, scale=-0.5))

            def keep_hidden(j):
                if not (isinstance(j, int) and j == 0):
                    turned_h.wait(act, j - 1, "h")
                for i in range(2):
                    first_mm.wait(act, j, str(i))
                    hid_ok.inc(str(i), A(hid[:, i * 512:(i + 1) * 512], hid_ps[i][:, :], ACT.Copy))

            b1f = b1.rearrange("p e t -> p (e t)")

            def relu(j):
                e = expert_of(j)
                if not (isinstance(j, int) and j == 0):
                    second_mm.wait(act, j - 1, "y")
                turned_h.wait(act, j, "h")
                for t in range(FT // 2):
                    relu_act.inc(str(t), A(hidT[:, t], hidT_ps[0][:, t * P:(t + 1) * P], ACT.Relu,
                                           bias=b1f[:, bass.ds(e * FT + t, 1)]))

            route.wait(act, 0, "expert")
            root(prep_act, prep, 0, 0)
            root(prep_act, prep, 1, 0)
            keep_hidden(0)

            def iteration(j, s):
                known = isinstance(j, int)
                relu(j)
                if not (known and j == 0):
                    root(fin_act, fin, j - 1, 1)
                if not (known and j + 2 >= EBLK):
                    root(prep_act, prep, j + 2, 0)
                if not (known and j + 1 >= EBLK):
                    keep_hidden(j + 1)

            for s in range(DEPTH):
                iteration(s, s)
            with act.Fori(1, EBLK // DEPTH - 1) as i:
                for s in range(DEPTH):
                    iteration(i * DEPTH + s, s)
            for s in range(DEPTH):
                iteration(EBLK - DEPTH + s, s)
            root(fin_act, fin, EBLK - 1, 1)

        @block.vector
        def _(dve):
            TT, STT = nc.vector.tensor_tensor, nc.vector.scalar_tensor_tensor
            nc.vector.memset(ones, 1.0).then_inc(const_ok, 1)
            nc.vector.memset(tiny, TINY).then_inc(const_ok, 1)
            nc.vector.memset(gneps, GN_EPS).then_inc(const_ok, 1)
            nc.vector.memset(lneps, LN_EPS).then_inc(const_ok, 1)
            nc.vector.memset(Wt[:, :, :, 0:1], 1.0).then_inc(const_ok, 1)
            dve.wait_ge(w_in, 16 * d["_nloads"])
            i = PARAMS.index("misc_a")
            nc.vector.tensor_scalar(negp, par[:, i, :], -1.0, None, ALU.mult).then_inc(const_ok, 1)
            dve.wait_ge(const_ok, 6)

            def mix_stage(m):
                dve.wait_ge(xT_in, (m + 1) * 32)
                if not (isinstance(m, int) and m == 0):
                    comb.wait(dve, m - 1, "u1")
                    ring.wait_full(dve, m - 1, "v1")
                mixed.inc("dx", TT(bt(dx), x_prev, x_now, ALU.subtract))
                mixed.wait(dve, m, "dx")
                for h in range(HALF):
                    mixed.inc(f"mix{h}", STT(out=bt(mix)[:, h], in0=bt(dx)[:, h], scalar=prm("maa_x", h), in1=x_now[:, h],
                                            op0=ALU.mult, op1=ALU.add))

            def xm_stage(m):
                if not (isinstance(m, int) and m == 0):
                    ring.wait_full(dve, m - 1, "rk1")
                    comb_act.wait(dve, m - 1, "iW")
                    comb.wait(dve, m - 1, "u1")
                for g in range(4):
                    for h in range(HALF):
                        nm = f"lo2_{g}{h}"
                        ring.wait_full(dve, m, nm)
                        ins = STT(out=xm[g][:, h], in0=ring.tile(nm)[:, :], scalar=prm(f"maa{g}", h), in1=dx[:, h],
                                  op0=ALU.add, op1=ALU.mult)
                        xm_ok.inc(f"{g}{h}", ins)

            def decays(m):
                first = isinstance(m, int) and m == 0

                def do(step, ins):
                    comb.inc(step, ins)

                def after(step):
                    comb.wait(dve, m, step)

                proj.wait(dve, m, "ln")
                do("ls", STT(out=zt, in0=zt, scalar=0.0, in1=t1, op0=ALU.min, op1=ALU.subtract))
                after("ls")
                do("e2", STT(out=mk, in0=zt, scalar=-0.5, in1=mk, op0=ALU.add, op1=ALU.mult))
                ring.wait_full(dve, m, "r1")
                for h in range(HALF):
                    for b in range(B):
                        do(f"scan{h * B + b}", nc.vector.tensor_tensor_scan(bt(L)[:, h, b], ones, Wt[:, h, b, 1:TB + 1], 0.0,
                                                                           ALU.mult, ALU.add))

            def combine(m):
                first = isinstance(m, int) and m == 0

                def do(step, ins):
                    comb.inc(step, ins)

                def after(step):
                    comb.wait(dve, m, step)

                proj.wait(dve, m, "inv")
                do("kkn", STT(out=kk, in0=nrm, scalar=1e12, in1=kk, op0=ALU.min, op1=ALU.mult))
                do("t", TT(nma, at, nma, ALU.mult))
                after("t")
                do("f", TT(ma, nma, ma, ALU.add))
                after("f")
                do("k2", TT(kt, ma, kt, ALU.mult))
                do("bt", TT(at, kk, at, ALU.mult))
                comb_act.wait(dve, m, "ek")
                after("k2")
                do("k3", TT(kt, kt, mk, ALU.mult))
                after("k3")
                for h in range(HALF):
                    do(f"rk{h}", STT(out=rkt[:, h], in0=rt[:, h], scalar=prm("faaaa", h), in1=kt[:, h],
                                     op0=ALU.mult, op1=ALU.mult))
                do("ao", TT(ao[:, :, :, 0:TB], bt(kk), Wt[:, :, :, 0:TB], ALU.mult))
                do("aend", nc.vector.tensor_copy(ao[:, :, :, TB:TB + 1], Wt[:, :, :, TB:TB + 1]))
                after("rk1")
                do("q", TT(bt(rt), bt(rt), Wt[:, :, :, 1:TB + 1], ALU.mult))
                do("b", STT(out=at, in0=at, scalar=-1.0, in1=iW, op0=ALU.mult, op1=ALU.mult))
                do("k", TT(kt, kt, iW, ALU.mult))
                if not first:
                    handed.wait(dve, m - 1, "up")
                for h in range(HALF):
                    ring.wait_full(dve, m, f"rk{h}")
                    ins = TT(ut[:, h], ring.tile(f"rk{h}")[:, :], vt[:, h], ALU.mult)
                    do(f"u{h}", ins)

            def normed(m):
                post_act.wait(dve, m, "rstd")
                post_dve.inc("n", TT(yc, yc, ysq, ALU.mult))
                handed.wait(dve, m, "up")
                post_dve.wait(dve, m, "n")
                for h in range(HALF):
                    post_dve.inc(f"w{h}", STT(out=yc[:, h], in0=yc[:, h], scalar=prm("ln_w", h), in1=up[:, h],
                                              op0=ALU.mult, op1=ALU.add))
                for h in range(HALF):
                    post_dve.wait(dve, m, f"w{h}")
                    post_dve.inc(f"g{h}", STT(out=yc[:, h], in0=yc[:, h], scalar=prm("ln_b", h), in1=gp[:, h],
                                              op0=ALU.add, op1=ALU.mult))

            def tokens(m):
                dve.wait_ge(xtok_in, (m + 1) * 32)
                for j in range(4):
                    w = f"wo{j // 2}"
                    post.wait_full(dve, m, w)
                    tok.inc(f"z{j}", TT(xtok[:, j], xtok[:, j], post.tile(w)[:, (j % 2) * C:(j % 2 + 1) * C], ALU.add))
                for j in range(4):
                    tok.wait(dve, m, f"z{j}")
                    tok.inc(f"st{j}", nc.vector.bn_stats(stats[:, j], xtok[:, j]))
                tok.wait(dve, m, "st3")
                tok.inc("settle", nc.vector.memset(spare, 0.0))
                for j in range(4):
                    tok.inc(f"ag{j}", nc.vector.bn_aggr(mv[:, j], stats[:, j]))
                rst.wait(dve, m, "exp")
                for j in range(4):
                    tok.inc(f"x1_{j}", nc.vector.tensor_scalar(xtok[:, j], xtok[:, j], mv[:, j, 0:1], rstd[:, j:j + 1],
                                                               ALU.subtract, ALU.mult))

            def keep_logits(m):
                post.wait_full(dve, m, "logit")
                ins = nc.vector.tensor_copy(logits[:, bass.ds(m * 4, 4), :],
                                            post.tile("logit")[:, 0:32].rearrange("p (j e) -> p j e", e=8))
                tok.inc("lg", ins)

            def y_reduce(blk, s, first):
                q = blk * SLOTS + s
                if s == 0 and not first:
                    dve.wait_ge(y_out, blk * 16)
                for g in range(4):
                    dve.wait_ge(qm_ok, q * 4 + g + 1)
                    t0 = s * SUB + 4 * g
                    nc.vector.tensor_reduce(ysb[:, :, t0:t0 + 4].rearrange("p i t -> p t i"),
                                            Sh[:, s % 2, 4 * g:4 * g + 4], AX.X, ALU.add).then_inc(yr_ok, 1)

            def hv(ap, h):
                return ap[:, 8 * h:8 * h + 8, :]

            def start_slot(blk, s, first):
                q = blk * SLOTS + s
                if first and s == 0:
                    nc.vector.memset(S0, 0.0).then_inc(s0_ok, 1)
                    return
                dve.wait_ge(s_ok, q * 32)
                prev = Sh[:, (s - 1) % 2, SUB - 1]
                if s == 0:
                    nc.vector.tensor_tensor(S0, prev, Wend[:, None, :].broadcast_to([P, HS, HS]), ALU.mult).then_inc(s0_ok, 1)
                else:
                    nc.vector.tensor_copy(S0, prev).then_inc(s0_ok, 1)

            def steps(blk, s):
                q = blk * SLOTS + s
                p = s % 2
                dve.wait_ge(relayed, (q + 1) * 2)
                for t in range(SUB):
                    prev = S0 if t == 0 else Sh[:, p, t - 1]
                    a = ab[p][:, 0, t, None, :].broadcast_to([P, 8, HS])
                    b = ab[p][:, 1, t, None, :].broadcast_to([P, 8, HS])
                    for h in range(2):
                        if t == 0:
                            dve.wait_ge(s0_ok, q + 1)
                        else:
                            dve.wait_ge(s_ok, q * 32 + 2 * (t - 1) + h + 1)
                        TT(hv(M, h), hv(prev, h), a, ALU.mult).then_inc(chain, 1)
                    for h in range(2):
                        dve.wait_ge(chain, q * 96 + t * 6 + h + 1)
                        nc.vector.tensor_reduce(SA[:, 8 * h:8 * h + 8], hv(M, h), AX.X, ALU.add).then_inc(chain, 1)
                    for h in range(2):
                        dve.wait_ge(chain, q * 96 + t * 6 + h + 3)
                        TT(hv(outer, h), SA[:, 8 * h:8 * h + 8, None].broadcast_to([P, 8, HS]), b, ALU.mult).then_inc(chain, 1)
                    dve.wait_ge(z_ok, q * SUB + t + 1)
                    for h in range(2):
                        dve.wait_ge(chain, q * 96 + t * 6 + h + 5)
                        TT(hv(Sh[:, p, t], h), hv(outer, h), hv(Z[:, t % 2], h), ALU.add).then_inc(s_ok, 1)

            mix_stage(0)
            xm_stage(0)
            decays(0)
            combine(0)
            mix_stage(1)

            def body(n, first, ahead):
                start_slot(n, 0, first)
                if not first:
                    y_reduce(n - 1, 2, False)
                if ahead:
                    xm_stage(n + 1)
                steps(n, 0)
                start_slot(n, 1, False)
                if not first:
                    y_reduce(n - 1, 3, False)
                if ahead:
                    decays(n + 1)
                steps(n, 1)
                start_slot(n, 2, False)
                y_reduce(n, 0, first)
                if not first:
                    normed(n - 1)
                if ahead:
                    combine(n + 1)
                steps(n, 2)
                start_slot(n, 3, False)
                y_reduce(n, 1, False)
                if ahead == 2:
                    mix_stage(n + 2)
                if not first:
                    tokens(n - 1)
                steps(n, 3)
                if not first:
                    keep_logits(n - 1)

            body(0, True, 2)
            with dve.Fori(1, last - 1) as n:
                body(n, False, 2)
            body(last - 1, False, 1)
            body(last, False, 0)
            y_reduce(last, 2, False)
            y_reduce(last, 3, False)
            normed(last)
            tokens(last)
            keep_logits(last)

            dve.wait_ge(route_in, 48)
            R = lambda name: route.wait(dve, 0, name)
            tok.wait(dve, last, "lg")
            red = nc.vector.tensor_reduce
            b3 = lambda ap: ap[:, :, None].broadcast_to([P, NTILE, E])
            route.inc("max", red(best, logits, AX.X, ALU.max))
            R("max")
            route.inc("eq", TT(onehot, logits, b3(best), ALU.is_ge))
            R("eq")
            route.inc("code", TT(onehot, onehot, cst["prefer"][:, None, :].broadcast_to([P, NTILE, E]), ALU.mult))
            R("code")
            route.inc("cmax", red(best, onehot, AX.X, ALU.max))
            R("cmax")
            route.inc("onehot", TT(onehot, onehot, b3(best), ALU.is_equal))
            route_pe.wait(dve, 0, "rank")
            rank = ne(route_ps[0][:, 0:NTILE * E])
            totals = route_ps[1][:, 0:NTILE * E].rearrange("p (n e) -> p e n", e=E)
            route.inc("sum", nc.vector.tensor_copy(place, rank))
            for e in range(E):
                route.inc(f"run{e}", nc.vector.tensor_tensor_scan(run[:, e], ones[:, 0:NTILE], totals[:, e], 0.0, ALU.mult, ALU.add))
            R(f"run{E - 1}")
            c2 = cmp[:, 0:E * NTILE].rearrange("p (e n) -> p e n", e=E)
            route.inc("cnt", TT(c2, run[:, :, NTILE - 1:NTILE].broadcast_to([P, E, NTILE]),
                                cst["fill"][:, None, :].broadcast_to([P, E, NTILE]), ALU.is_gt))
            R("cnt")
            route.inc("nblk", red(blocks, c2, AX.X, ALU.add))
            R("nblk")
            route.inc("bend", nc.vector.tensor_tensor_scan(blk_end, ones[:, 0:E], blocks, 0.0, ALU.mult, ALU.add))
            R("bend")
            route.inc("bstart", TT(blocks, blk_end, blocks, ALU.subtract))
            route.inc("excl", TT(run, run, totals, ALU.subtract))
            R("excl")
            route.inc("p1", TT(place, place, run.rearrange("p e n -> p n e"), ALU.add))
            R("p1")
            route.inc("p2", STT(out=place, in0=blocks[:, None, :].broadcast_to([P, NTILE, E]), scalar=float(P), in1=place,
                                op0=ALU.mult, op1=ALU.add))
            R("p2")
            route.inc("p3", TT(place, place, onehot, ALU.mult))
            R("p3")
            route.inc("pos", red(posf, place, AX.X, ALU.add))
            R("pos")
            route.inc("posi", nc.vector.tensor_copy(posi, posf))
            R("posi")
            route.inc("slot", nc.vector.tensor_scalar(slotp, posi, P - 1, None, ALU.bitwise_and))
            route.inc("blk", nc.vector.tensor_scalar(blki, posi, P.bit_length() - 1, None, ALU.logical_shift_right))
            R("blk")
            route.inc("slotf", nc.vector.tensor_copy(slotf, slotp))
            route.inc("blkf", nc.vector.tensor_copy(blkf, blki))
            c3 = cmp[:, 0:EBLK * E].rearrange("p (j e) -> p j e", e=E)
            route.inc("ecmp", TT(c3, cst["eblock"][:, :, None].broadcast_to([P, EBLK, E]),
                                 blk_end[:, None, :].broadcast_to([P, EBLK, E]), ALU.is_ge))
            R("ecmp")
            route.inc("esum", red(efl, c3, AX.X, ALU.add))
            R("esum")
            route.inc("expert", nc.vector.tensor_scalar(expert, efl, float(E - 1), None, ALU.min))
            for n in range(NTILE):
                if n >= RSEL:
                    dve.wait_ge(sel_used, n - RSEL + 1)
                nc.vector.tensor_scalar(in_slot[:, n % RSEL], cst["slot"], slotf[:, n:n + 1], None, ALU.is_equal)
                nc.vector.tensor_scalar(in_blk[:, n % RSEL], cst["eblock"], blkf[:, n:n + 1], cst["row"][:, n:n + 1],
                                        ALU.is_equal, ALU.mult).then_inc(sel_ok, 1)
            route_pe.wait(dve, 0, "table")
            nc.vector.tensor_scalar(table, route_ps[2][:, 0:EBLK], float(NTOK), None, ALU.add).then_inc(table_ok, 1)

            def expert_of(j):
                return dve.value_load(expert[0:1, bass.ds(j, 1)], min_val=0, max_val=E - 1)

            def row(w, e):
                return view(at_rows + w * E * D, E * D)[:, bass.ds(e * D, D)]

            def prepare(j, s):
                known = isinstance(j, int)
                if known:
                    dve.wait_ge(gathered[s], 16 * (j // DEPTH + 1))
                else:
                    dve.wait_ge(gathered[s], round_of(j, s) * 16)
                prep.inc("st", nc.vector.bn_stats(estat[:, 0], xg[:, s]))
                prep.wait(dve, j, "st")
                prep.inc("settle", nc.vector.memset(spare, 0.0))
                prep.inc("ag", nc.vector.bn_aggr(emv[:, 0], estat[:, 0]))
                e = expert_of(j)
                if not (known and j == 0):
                    turned_x.wait(dve, j - 1, "x")
                prep_act.wait(dve, j, "exp")
                prep.inc("xh", nc.vector.tensor_scalar(xn, xg[:, s], emv[:, 0, 0:1], erstd[:, 0:1], ALU.subtract, ALU.mult))
                prep.wait(dve, j, "xh")
                prep.inc("g", TT(xn, xn, row(0, e), ALU.mult))
                prep.wait(dve, j, "g")
                prep.inc("l", TT(xn, xn, row(1, e), ALU.add))
                prep.inc("zb", STT(out=zb[:, s], in0=xg[:, s], scalar=2.0, in1=row(2, e), op0=ALU.mult, op1=ALU.add))

            def keep_xnT(j):
                if not (isinstance(j, int) and j == 0):
                    first_mm.wait(dve, j - 1, "1")
                turned_x.wait(dve, j, "x")
                xnT_ok.inc("x", nc.vector.tensor_copy(xnT, xnT_ps[:, 0:D].rearrange("p (k n) -> p k n", k=HALF)))

            b1f = b1.rearrange("p e t -> p (e t)")

            def relu(j):
                e = expert_of(j)
                if not (isinstance(j, int) and j == 0):
                    second_mm.wait(dve, j - 1, "y")
                turned_h.wait(dve, j, "h")
                for t in range(FT // 2, FT):
                    relu_dve.inc(str(t), nc.vector.tensor_scalar(hidT[:, t], hidT_ps[1][:, (t - 4) * P:(t - 3) * P],
                                                                 b1f[:, bass.ds(e * FT + t, 1)], 0.0, ALU.add, ALU.max))

            def finish(j, s):
                second_mm.wait(dve, j, "y")
                fin.inc("z", TT(zb[:, s], zb[:, s], y_ps[s][:, 0:D], ALU.add))
                fin.wait(dve, j, "z")
                fin.inc("st", nc.vector.bn_stats(estat[:, 1], zb[:, s]))
                fin.wait(dve, j, "st")
                fin.inc("settle", nc.vector.memset(spare, 0.0))
                fin.inc("ag", nc.vector.bn_aggr(emv[:, 1], estat[:, 1]))
                if not (isinstance(j, int) and j < DEPTH):
                    dve.wait_ge(scattered[s], (round_of(j, s) - 1) * 16)
                fin_act.wait(dve, j, "exp")
                fin.inc("o", nc.vector.tensor_scalar(ob[:, s], zb[:, s], emv[:, 1, 0:1], erstd[:, 1:2], ALU.subtract, ALU.mult))

            rounds = {}

            def round_of(j, s):
                return j // DEPTH + 1 if isinstance(j, int) else rounds[0] + (j_off[0] // DEPTH) + 1

            j_off = [0]
            dve.wait_ge(rows_in, 48)
            prepare(0, 0)
            keep_xnT(0)
            prepare(1, 1)
            keep_xnT(1)

            def iteration(j, s, i=None):
                rounds[0] = i
                known = isinstance(j, int)
                relu(j)
                if not (known and j == 0):
                    j_off[0] = s - 1 if s else -1
                    finish(j - 1, (s - 1) % DEPTH)
                if not (known and j + 2 >= EBLK):
                    j_off[0] = s + 2
                    prepare(j + 2, (s + 2) % DEPTH)
                    keep_xnT(j + 2)

            for j in range(2 * DEPTH):
                iteration(j, j % DEPTH)
            with dve.Fori(2, EBLK // DEPTH - 1) as i:
                for s in range(DEPTH):
                    iteration(i * DEPTH + s, s, i)
            for s in range(DEPTH):
                iteration(EBLK - DEPTH + s, s)
            finish(EBLK - 1, DEPTH - 1)

        @block.gpsimd
        def _(pool):
            TT = nc.gpsimd.tensor_tensor

            def outer_vk(blk, s, t0, nt):
                p = s % 2
                k = kqv[:, p, 0, t0:t0 + nt, None, :].broadcast_to([P, nt, HS, HS])
                v = kqv[:, p, 2, t0:t0 + nt, :, None].broadcast_to([P, nt, HS, HS])
                TT(VK[:, t0 % 8:t0 % 8 + nt], v, k, ALU.mult).then_inc(vk_ok, 1)

            def times_q(blk, s):
                p = s % 2
                for g in range(4):
                    q = kqv[:, p, 1, 4 * g:4 * g + 4, None, :].broadcast_to([P, 4, HS, HS])
                    TT(Sh[:, p, 4 * g:4 * g + 4], Sh[:, p, 4 * g:4 * g + 4], q, ALU.mult).then_inc(qm_ok, 1)

            def slot(blk, s, first):
                q = blk * SLOTS + s
                pool.wait_ge(relayed, (q + 1) * 2)
                if not (first and s == 0):
                    pool.wait_ge(z_ok, q * SUB)
                outer_vk(blk, s, 0, 4)
                pool.wait_ge(s0_ok, q + 1)
                if not (first and s == 0):
                    times_q(blk, (s - 1) % SLOTS)
                for t in range(SUB):
                    pool.wait_ge(vk_ok, q * 13 + (1 if t < 4 else t - 2))
                    if t:
                        pool.wait_ge(s_ok, q * 32 + 2 * t)
                    TT(Z[:, t % 2], S0 if t == 0 else Sh[:, s % 2, t - 1], VK[:, t % 8], ALU.add).then_inc(z_ok, 1)
                    if t < 12:
                        outer_vk(blk, s, t + 4, 1)

            for s in range(SLOTS):
                slot(0, s, True)
            with pool.Fori(1, NBLK) as n:
                for s in range(SLOTS):
                    slot(n, s, False)
            pool.wait_ge(s_ok, NBLK * SLOTS * 32)
            times_q(last, 3)

            x_rows = x1d.rearrange("b t c -> (b t) c")
            out_rows = out.rearrange("b t c -> (b t) c")
            pool.wait_ge(table_ok, 1)
            pool.wait_ge(x1_out, NBLK * 32)
            nc.gpsimd.memset(xg, 0.0).then_inc(xg_clear, 1)
            pool.wait_ge(xg_clear, 1)

            w = Waits(pool, carrier_pool)

            def gather(j, s):
                if not (isinstance(j, int) and j < DEPTH):
                    prep.wait(w, j - DEPTH, "zb")
                idx_ok.inc("gather", nc.gpsimd.tensor_copy(gidx[:, s:s + 1], table[:, bass.ds(j, 1)]))
                idx_ok.wait(w, j, "gather")
                nc.gpsimd.indirect_dma_start(out=xg[:, s], out_offset=None, in_=x_rows,
                                             in_offset=bass.IndirectOffsetOnAxis(ap=gidx[:, s:s + 1], axis=0),
                                             bounds_check=NTOK - 1, oob_is_err=False).then_inc(gathered[s], 16)

            def scatter(j, s):
                fin.wait(w, j, "o")
                sidx_ok.inc("scatter", nc.gpsimd.tensor_copy(sidx[:, s:s + 1], table[:, bass.ds(j, 1)]))
                sidx_ok.wait(w, j, "scatter")
                nc.gpsimd.indirect_dma_start(out=out_rows, out_offset=bass.IndirectOffsetOnAxis(ap=sidx[:, s:s + 1], axis=0),
                                             in_=ob[:, s], in_offset=None,
                                             bounds_check=NTOK - 1, oob_is_err=False).then_inc(scattered[s], 16)

            for s in range(DEPTH):
                gather(s, s)

            def iteration(j, s):
                if not (isinstance(j, int) and j + DEPTH >= EBLK):
                    gather(j + DEPTH, s)
                if not (isinstance(j, int) and j == 0):
                    scatter(j - 1, (s - 1) % DEPTH)

            for s in range(DEPTH):
                iteration(s, s)
            with pool.Fori(1, EBLK // DEPTH - 1) as i:
                for s in range(DEPTH):
                    iteration(i * DEPTH + s, s)
            for s in range(DEPTH):
                iteration(EBLK - DEPTH + s, s)
            scatter(EBLK - 1, DEPTH - 1)
            for s in range(DEPTH):
                pool.wait_ge(scattered[s], EBLK // DEPTH * 16)


def layout(inputs):
    import numpy as np
    g = {k[len("L0_attn_"):]: np.asarray(v) for k, v in inputs.items() if k.startswith("L0_attn_")}
    f = {k[len("L0_ffn_"):]: np.asarray(v) for k, v in inputs.items() if k.startswith("L0_ffn_")}
    xTp = np.zeros((C, B, T + 1), np.float32)
    xTp[:, :, 1:] = g["x"].transpose(2, 0, 1)
    out1 = np.zeros((3, 96, C), np.float32)
    out1[0, 0:64], out1[1, 64:80], out1[2, 80:96] = g["decay_w2"], g["aaa_w2"], g["ma_w2"]
    out2 = np.zeros((2, 64, C), np.float32)
    out2[0, 0:16], out2[1, 32:48] = g["kkk_w2"], g["mk_w2"]
    h2T = np.zeros((C, 64), np.float32)
    h2T[:, 0:16], h2T[:, 32:48] = g["kkk_w1"].T, g["mk_w1"].T
    i = np.arange(P)
    same = (i[:, None] // HS == i[None, :] // HS).astype(np.float32)
    eye = np.eye(P, dtype=np.float32)
    cc = np.ascontiguousarray
    tile, part = np.arange(NTILE)[None, :], i[:, None]
    row = (2 * (tile % 4) + part // TB) * T + (tile // 4) * TB + part % TB
    wide = lambda v: np.broadcast_to(np.asarray(v)[None, :], (P, len(v)))
    cst = {"slot": wide(np.arange(P)), "eblock": wide(np.arange(EBLK)), "prefer": wide(E - np.arange(E)),
           "fill": wide(P * np.arange(NTILE)), "row": row - NTOK}
    return {
        "x": cc(g["x"]), "xTp": xTp,
        "WrT": cc(g["Wr"].T), "WkT": cc(g["Wk"].T), "WvT": cc(g["Wv"].T), "WoT": cc(g["Wo"].T),
        "maa1T": cc(g["maa_w1"].T), "maa2": cc(g["maa_w2"].reshape(P, C)),
        "gate1T": cc(g["gate_w1"].T), "gate2": cc(g["gate_w2"]),
        "h1T": cc(np.concatenate([g["decay_w1"].T, g["aaa_w1"].T, g["ma_w1"].T], axis=1)), "h2T": h2T,
        "out1": out1, "out2": out2,
        "mats": np.stack([same, same / HS, eye - same / HS, eye]).astype(np.float32),
        "centT": cc(f["centroids"].T),
        "mats2": np.stack([i[:, None] < i[None, :], np.ones((P, P), bool)]).astype(np.float32),
        "cst": np.concatenate([cst[n] for n in CONSTS], axis=1).astype(np.float32),
        "W1": cc(f["W1"]), "W2": cc(f["W2"]), "b1T": cc(f["b1"].reshape(E * FT, P).T),
        "ln_g": cc(f["ln_g"].reshape(-1)), "ln_b": cc(f["ln_b"].reshape(-1)), "b2": cc(f["b2"].reshape(-1)),
        "par": cc(np.stack([g["time_maa_x"]] + [g["time_maa"].reshape(4, C)[k] for k in range(4)]
                           + [g["time_decay"], g["time_aaaaa"], g["time_misc_a"], g["time_misc_k"], g["time_faaaa"],
                              g["ln_w"], g["ln_b"]]).reshape(len(PARAMS), HALF, P).transpose(2, 0, 1)),
    }


def kernel(**inputs):
    import concourse.bacc as bacc
    from concourse.bass_utils import run_bass_kernel_spmd as run

    nc = bacc.Bacc("TRN2", target_bir_lowering=False, num_devices=1)
    arrays = layout(inputs)
    d = {n: nc.dram_tensor(f"in_{n}", a.shape, mybir.dt.from_np(a.dtype), kind="ExternalInput").ap() for n, a in arrays.items()}
    d["_nloads"] = 15
    out = nc.dram_tensor("out_0_dram", (B, T, C), F32, kind="ExternalOutput").ap()
    build(nc, d, out)
    r = run(nc, [{f"in_{n}": a for n, a in arrays.items()}], core_ids=[0])
    return r.results[0]["out_0_dram"]
```

```python
from contextlib import ExitStack

import concourse.bass as bass
from concourse import mybir

F32 = mybir.dt.float32
I32 = mybir.dt.int32
ALU = mybir.AluOpType
ACT = mybir.ActivationFunctionType
AX = mybir.AxisListType

P = 128
B, T, C = 8, 512, 256
HS = 16
H = C // HS
TB = 64
NBLK = T // TB
COLS = B * TB
SUB = 16
SLOTS = TB // SUB
Q_BEFORE = [(0, 4), (4, 4), (8, 2)]
Q_BETWEEN = {2 * i: (10 + i, 1) for i in range(6)}
Q_PARTS = len(Q_BEFORE) + len(Q_BETWEEN)
HALF = C // P
GN_EPS = 0.00064
LN_EPS = 1e-05
DECAY = 0.6065306597126334
TINY = 1e-37
E, D, F = 8, C, 1024
FT = F // P
NTOK = B * T
NTILE = NTOK // P
EBLK = NTILE + E - 1
DEPTH = 3
assert EBLK % DEPTH == 0
CONSTS = {"slot": P, "eblock": EBLK, "prefer": E, "fill": NTILE, "row": NTILE}
PARAMS = ["maa_x", "maa0", "maa1", "maa2", "maa3", "decay", "aaaaa", "misc_a", "misc_k", "faaaa", "ln_w", "ln_b"]


class Steps:

    def __init__(self, sem, names):
        self.sem, self.names, self.seen = sem, names, 0

    def inc(self, name, ins):
        assert self.names[self.seen % len(self.names)] == name, (name, self.names[self.seen % len(self.names)])
        self.seen += 1
        return ins.then_inc(self.sem, 1)

    def value(self, blk, name):
        return blk * len(self.names) + self.names.index(name) + 1

    def wait(self, eng, blk, name):
        eng.wait_ge(self.sem, self.value(blk, name))


RING = 4
RING_JOBS = (["lo1"] + [f"lo2_{g}{h}" for g in range(4) for h in range(2)]
             + ["h1", "h2", "z0", "z1", "mk0", "mk1", "tg", "r0", "r1", "k0", "k1", "v0", "v1", "kk0", "kk1",
                "a0", "a1", "ma0", "ma1", "ss0", "ss1", "g0", "g1", "rk0", "rk1"])
POST_JOBS = ["yc0", "yc1", "var0", "var1", "wo0", "wo1", "xT0", "xT1", "logit"]


class Banks:

    def __init__(self, banks, jobs, filled, emptied_by):
        self.banks, self.jobs, self.filled, self.emptied_by = banks, jobs, filled, emptied_by

    def where(self, name):
        j = self.jobs.index(name)
        return j % len(self.banks), j

    def tile(self, name):
        return self.banks[self.where(name)[0]]

    def wait_empty(self, eng, blk, name, first):
        b, j = self.where(name)
        if j >= len(self.banks):
            steps, step = self.emptied_by[self.jobs[j - len(self.banks)]]
            steps.wait(eng, blk, step)
        elif not first:
            steps, step = self.emptied_by[self.jobs[b::len(self.banks)][-1]]
            steps.wait(eng, blk - 1, step)

    def fill(self, name, ins):
        return ins.then_inc(self.filled[self.where(name)[0]], 1)

    def wait_full(self, eng, blk, name):
        b, j = self.where(name)
        eng.wait_ge(self.filled[b], blk * len(self.jobs[b::len(self.banks)]) + j // len(self.banks) + 1)


class Waits:

    def __init__(self, eng, carrier):
        self.eng, self.carrier = eng, carrier

    def wait_ge(self, s, value):
        self.eng.wait_ge(s, value)
        if not isinstance(value, int):
            self.eng.sem_inc(self.carrier, 1)


def build(nc, d, out):
    with ExitStack() as ctx:
        sem = lambda name: ctx.enter_context(nc.semaphore(name))
        WORDS = 53208
        arena = ctx.enter_context(nc.sbuf_tensor("arena", [P, WORDS], F32))
        top = [0]

        def take(words):
            at = top[0]
            top[0] += words
            assert top[0] <= WORDS, top[0]
            return arena[:, at:at + words]

        def ct(ap=None):
            return (take(HALF * COLS) if ap is None else ap).rearrange("p (h n) -> p h n", h=HALF)

        def bt(ap):
            return ap.rearrange("p h (b t) -> p h b t", b=B)

        banks = [ctx.enter_context(nc.psum_tensor(f"bank{i}", [P, 512], F32)) for i in range(5)]
        ab_bank = [ctx.enter_context(nc.psum_tensor(f"ab{i}", [P, 512], F32)) for i in range(2)]
        ab = [b[:, :].rearrange("p (x t j) -> p x t j", x=2, t=SUB) for b in ab_bank]
        outer_bank = ctx.enter_context(nc.psum_tensor("outer", [P, 512], F32))
        outer = outer_bank[:, 0:HS * HS].rearrange("p (i j) -> p i j", i=HS)
        y_sum = banks[4][:, 0:HS * HS].rearrange("p (t i) -> p t i", t=SUB)
        hid_ps = banks[0:2]
        hidT_ps = banks[2:4]
        xnT_ps = banks[4]
        y_ps = [ab_bank[0], ab_bank[1], outer_bank]
        route_ps = banks[0:3]

        w_sq = take(4 * HALF * C).rearrange("p (w k n) -> p w k n", w=4, k=HALF)
        w_maa1 = take(HALF * P).rearrange("p (k n) -> p k n", k=HALF)
        w_maa2 = take(C)
        w_gate1 = take(HALF * P).rearrange("p (k n) -> p k n", k=HALF)
        w_gate2 = take(C)
        w_h1 = take(HALF * 96).rearrange("p (k n) -> p k n", k=HALF)
        w_h2 = take(HALF * 64).rearrange("p (k n) -> p k n", k=HALF)
        w_out1 = take(3 * C)[0:96, :].rearrange("p (w n) -> p w n", w=3)
        w_out2 = take(2 * C)[0:64, :].rearrange("p (w n) -> p w n", w=2)
        mats = take(4 * P).rearrange("p (m n) -> p m n", m=4)
        head_sum, head_mean, centre, ident = (mats[:, i, :] for i in range(4))
        cent = take(HALF * 8).rearrange("p (k e) -> p k e", k=HALF)
        par = take(len(PARAMS) * HALF).rearrange("p (w h) -> p w h", h=HALF)
        negp = take(HALF)
        tiny = take(1)
        gneps = take(1)
        lneps = take(1)
        spare = take(1)
        ones = take(TB)
        logits = take(NTILE * 8).rearrange("p (n e) -> p n e", e=8)

        def prm(name, h):
            i = PARAMS.index(name)
            return par[:, i, h:h + 1]

        at_proj = top[0]
        xT = take(HALF * B * (TB + 1)).rearrange("p (h b t) -> p h b t", h=HALF, b=B)
        x_now, x_prev = xT[:, :, :, 1:TB + 1], xT[:, :, :, 0:TB]
        dx = ct()
        zt = dx
        xm = [ct() for _ in range(4)]
        L, iW, rkt = xm[0], xm[1], xm[2]
        sg = iW
        lo1 = take(COLS)
        h1 = lo1
        h2 = take(COLS)
        tg = take(COLS)
        ao_flat = take(HALF * B * (TB + 1))
        ao = ao_flat.rearrange("p (h b t) -> p h b t", h=HALF, b=B)
        nrm = ct(ao_flat[:, 0:HALF * COLS])
        kk, rt, kt, vt, at, ma, nma, mk, t1 = (ct() for _ in range(9))
        Wt = take(HALF * B * (TB + 1)).rearrange("p (h b t) -> p h b t", h=HALF, b=B)
        gt, gp, ut, up = (ct() for _ in range(4))
        at_rec = top[0]
        PA = take(HS * (TB + 1)).rearrange("p (c t) -> p c t", c=HS)
        PX = take(4 * HS * TB).rearrange("p (x c t) -> p x c t", x=4, c=HS)
        kqv = take(2 * 3 * SUB * HS).rearrange("p (s x t c) -> p s x t c", s=2, x=3, t=SUB)
        Sh = take(2 * SUB * HS * HS).rearrange("p (s t i j) -> p s t i j", s=2, t=SUB, i=HS)
        VK = take(8 * HS * HS).rearrange("p (t i j) -> p t i j", t=8, i=HS)
        S0 = take(HS * HS).rearrange("p (i j) -> p i j", i=HS)
        Z = take(2 * HS * HS).rearrange("p (t i j) -> p t i j", t=2, i=HS)
        M = take(HS * HS).rearrange("p (i j) -> p i j", i=HS)
        SA = take(HS)
        Wend = take(HS)
        ysb = take(HS * TB).rearrange("p (i t) -> p i t", i=HS)
        at_yc = top[0]
        yc = ct()
        ysq = ct()
        x1T = ct(ysq.rearrange("p h n -> p (h n)"))
        at_xtok = top[0]
        xtok = take(4 * C).rearrange("p (j c) -> p j c", j=4)
        stats = take(4 * 6).rearrange("p (j c) -> p j c", j=4)
        mv = take(4 * 2).rearrange("p (j c) -> p j c", j=4)
        std = take(4)
        def view(at, words):
            return arena[:, at:at + words]

        W1 = view(at_proj, E * HALF * F).rearrange("p (e k f) -> p e k f", e=E, k=HALF)
        at_rows = at_proj + E * HALF * F
        assert at_rows + 3 * E * D <= at_rec
        rows = view(at_rows, 3 * E * D).rearrange("p (w e n) -> p w e n", w=3, e=E)
        W2 = view(at_rec, E * FT * D).rearrange("p (e t n) -> p e t n", e=E, t=FT)
        hid = view(at_yc, F)
        hidT = view(at_yc + F, F).rearrange("p (t n) -> p t n", t=FT)
        xn = view(at_xtok, D)
        xnT = view(at_xtok + D, D).rearrange("p (k n) -> p k n", k=HALF)
        b1 = take(E * FT).rearrange("p (e t) -> p e t", e=E)
        table = take(EBLK).bitcast(I32)
        expert = take(EBLK).bitcast(I32)
        gidx = take(DEPTH).bitcast(I32)
        sidx = take(DEPTH).bitcast(I32)
        estat = take(2 * 6).rearrange("p (w s) -> p w s", w=2)
        emv = take(2 * 2).rearrange("p (w s) -> p w s", w=2)
        estd = take(2)
        at_blk = top[0]
        xg = take(DEPTH * D).rearrange("p (s n) -> p s n", s=DEPTH)
        zb = take(DEPTH * D).rearrange("p (s n) -> p s n", s=DEPTH)
        ob = take(DEPTH * D).rearrange("p (s n) -> p s n", s=DEPTH)
        w_maa1x = view(at_blk, HALF * P).rearrange("p (k n) -> p k n", k=HALF)
        within = view(at_blk + HALF * P, COLS)
        at_cst = 0
        tri = view(0, P)
        all_ones = view(P, P)
        cst, at_c = {}, 2 * P
        for n, w in CONSTS.items():
            cst[n] = view(at_c, w)
            at_c += w
        assert at_c <= 3 * HALF * C
        at_tmp = [at_blk]

        def tmp(words):
            v = view(at_tmp[0], words)
            at_tmp[0] += words
            assert at_tmp[0] <= top[0]
            return v

        ne = lambda ap: ap.rearrange("p (n e) -> p n e", e=E)
        onehot = ne(tmp(NTILE * E))
        place = ne(tmp(NTILE * E))
        run = tmp(NTILE * E).rearrange("p (e n) -> p e n", e=E)
        cmp = tmp(EBLK * E)
        best = tmp(NTILE)
        blocks = tmp(E)
        blk_end = tmp(E)
        posf, slotf, blkf = tmp(NTILE), tmp(NTILE), tmp(NTILE)
        posi, slotp, blki = tmp(NTILE).bitcast(I32), tmp(NTILE).bitcast(I32), tmp(NTILE).bitcast(I32)
        RSEL = 4
        in_blk = view(at_yc, NTILE * EBLK).rearrange("p (s n) -> p s n", s=NTILE)
        in_slot = [v.rearrange("p (s n) -> p s n", s=RSEL)
                   for v in (view(at_yc + NTILE * EBLK, RSEL * P), tmp(RSEL * P))]
        efl = tmp(EBLK)

        xd_a = nc.dram_tensor("scr_a", (B, C, TB + 1), F32, kind="Internal").ap()
        xd_x = nc.dram_tensor("scr_x", (4, B, C, TB), F32, kind="Internal").ap()
        yd = nc.dram_tensor("scr_y", (B, C, TB), F32, kind="Internal").ap()
        x1d = nc.dram_tensor("scr_x1", (B, T, C), F32, kind="Internal").ap()

        w_in = sem("weights_in")
        early_in = sem("early_in")
        carrier = sem("wait_carrier")
        carrier_pool = sem("wait_carrier_pool")
        const_ok = sem("const_ok")
        xT_in = sem("xT_in")
        mixed = Steps(sem("mixed"), ["dx"])
        with_x = sem("with_x")
        xm_ok = Steps(sem("xm_ok"), [f"{g}{h}" for g in range(4) for h in range(2)])
        lo_ok = Steps(sem("lo_ok"), ["lo1"])
        proj = Steps(sem("proj"), ["h1t", "h1c", "h2t", "h2c", "z0", "abs0", "sg0", "z1", "abs1", "sg1", "mk0", "mk1", "exp", "ln",
                                   "tg", "r0", "r1", "k0", "k1", "v0", "v1", "kk0", "sq0", "kk1", "sq1",
                                   "a0", "a1", "ma0", "nma0", "ma1", "nma1", "lnss0", "lnss1", "inv"])
        comb_act = Steps(sem("comb_act"), ["W", "iW", "ek", "g0", "g1"])
        comb = Steps(sem("comb"), ["ls", "e2"] + [f"scan{h}" for h in range(HALF)]
                     + ["kkn", "t", "bt", "f", "k2", "k3", "rk0", "rk1", "aend", "k", "u0", "u1"])
        comb_pool = Steps(sem("comb_pool"), ["ao", "b", "q"])
        handed = Steps(sem("handed"), ["gp", "up"])
        scr_out = sem("scr_out")
        pair_in = sem("pair_in")
        relayed = sem("relayed")
        s0_ok = sem("s0_ok")
        s_ok = sem("s_ok")
        chain = sem("chain")
        vk_ok = sem("vk_ok")
        z_ok = sem("z_ok")
        qm_ok = sem("qm_ok")
        y_summed = sem("y_summed")
        yr_ok = sem("y_kept")
        y_out = sem("y_out")
        y_in = sem("y_in")
        post_act = Steps(sem("post_act"), ["c0", "s0", "c1", "s1", "v0", "v1", "ln", "rstd", "x1T0", "x1T1", "lg"])
        post_dve = Steps(sem("post_dve"), ["n", "w0", "w1", "g0", "g1"])
        tok = Steps(sem("tok"), [f"z{j}" for j in range(4)] + [f"st{j}" for j in range(4)] + ["settle"]
                    + [f"ag{j}" for j in range(4)] + ["inv"]
                    + [f"x1_{j}" for j in range(4)])
        rst = Steps(sem("rst"), ["sqrt"])
        freed = {"lo1": (lo_ok, "lo1"), "h1": (proj, "h1c"), "h2": (proj, "h2c"), "tg": (proj, "tg")}
        for h in "01":
            freed.update({f"lo2_{g}{h}": (xm_ok, f"{g}{h}") for g in range(4)})
            freed.update({f"{n}{h}": (proj, f"{n}{h}") for n in ("r", "k", "v", "a", "mk")})
            freed.update({f"kk{h}": (proj, f"sq{h}"), f"ma{h}": (proj, f"nma{h}"), f"z{h}": (proj, f"sg{h}"),
                          f"ss{h}": (proj, f"lnss{h}"), f"g{h}": (comb_act, f"g{h}"), f"rk{h}": (comb, f"u{h}")})
        ring = Banks(banks[:RING], RING_JOBS, [sem(f"filled{i}") for i in range(RING)], freed)
        freed = {"wo0": (tok, "z1"), "wo1": (tok, "z3"), "logit": (post_act, "lg")}
        for h in "01":
            freed.update({f"yc{h}": (post_act, f"s{h}"), f"var{h}": (post_act, f"v{h}"), f"xT{h}": (post_act, f"x1T{h}")})
        post = Banks(banks[RING:], POST_JOBS, [sem("post_filled")], freed)
        xtok_in = sem("xtok_in")
        x1_out = sem("x1_out")

        route_in = sem("route_in")
        route = Steps(sem("route"), ["max", "eq", "code", "cmax", "onehot", "sum"] + [f"run{e}" for e in range(E)]
                      + ["cnt", "nblk", "bend", "bstart", "excl", "p1", "p2", "p3", "pos", "posi", "slot", "blk", "slotf", "blkf",
                         "ecmp", "esum", "expert", "inblk", "rows"])
        route_pe = Steps(sem("route_pe"), ["rank", "table"])
        sel_ok = sem("sel_ok")
        sel_used = sem("sel_used")
        table_ok = sem("table_ok")
        w1_in = [sem(f"w1_in{e}") for e in range(E)]
        w2_in = [sem(f"w2_in{e}") for e in range(E)]
        rows_in = sem("rows_in")
        xg_clear = sem("xg_clear")
        w1_ready = sem("w1_ready")
        w2_ready = sem("w2_ready")
        gathered = [sem(f"gathered{i}") for i in range(DEPTH)]
        idx_ok = Steps(sem("idx_ok"), ["gather"])
        sidx_ok = Steps(sem("sidx_ok"), ["scatter"])
        scattered = [sem(f"scattered{i}") for i in range(DEPTH)]
        prep = Steps(sem("prep"), ["st", "settle", "ag", "xh", "g", "l", "zb"])
        inverse = Steps(sem("inverse"), ["inv"])
        roots = Steps(sem("roots"), ["sqrt"])
        xnT_ok = Steps(sem("xnT_ok"), ["x"])
        hid_ok = Steps(sem("hid_ok"), ["0", "1"])
        relu_act = Steps(sem("relu_act"), [str(t) for t in range(FT // 2)])
        relu_dve = Steps(sem("relu_dve"), [str(t) for t in range(FT // 2, FT)])
        fin = Steps(sem("fin"), ["z", "st", "settle", "ag", "o"])
        turned_x = Steps(sem("turned_x"), ["x"])
        turned_h = Steps(sem("turned_h"), ["h"])
        first_mm = Steps(sem("first_mm"), ["0", "1"])
        second_mm = Steps(sem("second_mm"), ["y"])

        block = ctx.enter_context(nc.Block())
        last = NBLK - 1

        @block.sync
        def _(sp):
            w = Waits(sp, carrier)

            early = [(par, d["par"]), (w_maa1, d["maa1T"].rearrange("(k p) n -> p k n", p=P)), (w_maa2, d["maa2"])]
            loads = [(w_sq[:, i], d[n].rearrange("(k p) n -> p k n", p=P)) for i, n in enumerate(["WrT", "WkT", "WvT", "WoT"])]
            loads += [(w_gate1, d["gate1T"].rearrange("(k p) n -> p k n", p=P)), (w_gate2, d["gate2"]),
                      (w_h1, d["h1T"].rearrange("(k p) n -> p k n", p=P)), (w_h2, d["h2T"].rearrange("(k p) n -> p k n", p=P)),
                      (w_out1, d["out1"].rearrange("w p n -> p w n")), (w_out2, d["out2"].rearrange("w p n -> p w n")),
                      (mats, d["mats"].rearrange("m p n -> p m n")), (cent, d["centT"].rearrange("(k p) e -> p k e", p=P))]
            loads.sort(key=lambda pair: pair[0] is not w_h1 and pair[0] is not w_h2)

            def load_xT(m):
                for h in range(HALF):
                    sp.dma_start(xT[:, h], d["xTp"][h * P:(h + 1) * P, :, bass.ds(m * TB, TB + 1)]).then_inc(xT_in, 16)

            load_xT(0)
            for dst, src in early:
                sp.dma_start(dst, src).then_inc(early_in, 16)
            for dst, src in loads:
                sp.dma_start(dst, src).then_inc(w_in, 16)
            assert len(loads) == d["_nloads"]

            def next_xT(m):
                ring.wait_full(w, m - 1, "v1")
                mixed.wait(w, m - 1, "dx")
                load_xT(m)

            def y_turn(m):
                w.wait_ge(yr_ok, m * SLOTS + SLOTS)
                sp.dma_start(yd.rearrange("b (h i) t -> (b h) (i t)", h=H), ysb.rearrange("p i t -> p (i t)")).then_inc(y_out, 16)
                w.wait_ge(y_out, (m + 1) * 16)
                if not (isinstance(m, int) and m == 0):
                    post_wait_prev(sp, m)
                for h in range(HALF):
                    sp.dma_start(bt(yc)[:, h], yd[:, h * P:(h + 1) * P, :].rearrange("b p t -> p b t")).then_inc(y_in, 16)
                for e in range(2):
                    sp.dma_start(xtok[e * 64:(e + 1) * 64, :, :],
                                 d["x"][:, bass.ds(m * TB, TB), :].rearrange("(j e) t c -> e t j c", e=2)[e]
                                 ).then_inc(xtok_in, 16)

            def post_wait_prev(sp, m):
                post.wait_full(w, m - 1, "wo1")
                w.wait_ge(x1_out, m * 32)
                post.wait_full(w, m - 1, "xT1")

            def to_pairs(m):
                if not (isinstance(m, int) and m == 0):
                    w.wait_ge(pair_in, m * 80)
                for i, (src, step) in enumerate([(vt, None), (ao, "ao"), (at, "b"), (kt, "k"), (rt, "q")]):
                    if step is None:
                        proj.wait(w, m, "v1")
                    elif step == "k":
                        comb.wait(w, m, step)
                    else:
                        comb_pool.wait(w, m, step)
                        if step == "ao":
                            comb.wait(w, m, "aend")
                    x = {0: 2, 2: 3, 3: 0, 4: 1}.get(i)
                    for h in range(HALF):
                        if x is None:
                            sp.dma_start(xd_a[:, h * P:(h + 1) * P, :].rearrange("b p t -> p b t"), ao[:, h]).then_inc(scr_out, 16)
                        else:
                            sp.dma_start(xd_x[x, :, h * P:(h + 1) * P, :].rearrange("b p t -> p b t"), bt(src)[:, h]).then_inc(scr_out, 16)
                w.wait_ge(scr_out, (m + 1) * 160)
                if not (isinstance(m, int) and m == 0):
                    w.wait_ge(relayed, m * SLOTS * 2)
                sp.dma_start(PA.rearrange("p c t -> p (c t)"), xd_a.rearrange("b (h c) t -> (b h) (c t)", h=H)).then_inc(pair_in, 16)
                for x in range(4):
                    sp.dma_start(PX[:, x].rearrange("p c t -> p (c t)"),
                                 xd_x[x].rearrange("b (h c) t -> (b h) (c t)", h=H)).then_inc(pair_in, 16)

            def store_x1(m):
                tok.wait(w, m, "x1_3")
                for e in range(2):
                    sp.dma_start(x1d[:, bass.ds(m * TB, TB), :].rearrange("(j e) t c -> e t j c", e=2)[e],
                                 xtok[e * 64:(e + 1) * 64, :, :]).then_inc(x1_out, 16)

            next_xT(1)
            to_pairs(0)

            def body(n, first, ahead):
                if not first:
                    y_turn(n - 1)
                if ahead == 2:
                    next_xT(n + 2)
                if ahead:
                    to_pairs(n + 1)
                if not first:
                    store_x1(n - 1)

            body(0, True, 2)
            body(1, False, 2)
            with sp.Fori(2, last - 1) as n:
                body(n, False, 2)
            body(last - 1, False, 1)
            to_pairs_over = NBLK * 80
            w.wait_ge(pair_in, to_pairs_over)
            comb.wait(w, last, "u1")
            sp.dma_start(view(0, 2 * P).rearrange("p (m n) -> p m n", m=2), d["mats2"].rearrange("m p n -> p m n")).then_inc(route_in, 16)
            sp.dma_start(view(2 * P, sum(CONSTS.values())), d["cst"]).then_inc(route_in, 16)
            sp.dma_start(b1.rearrange("p e t -> p (e t)"), d["b1T"]).then_inc(route_in, 16)
            for e in range(E):
                sp.dma_start(W1[:, e], d["W1"][e].rearrange("(k p) f -> p k f", p=P)).then_inc(w1_in[e], 16)
            body(last, False, 0)
            y_turn(last)
            w.wait_ge(s_ok, NBLK * SLOTS * 32)
            w.wait_ge(yr_ok, NBLK * SLOTS)
            for e in range(E):
                sp.dma_start(W2[:, e], d["W2"][e].rearrange("(t p) n -> p t n", p=P)).then_inc(w2_in[e], 16)
            post_dve.wait(w, last, "g1")
            for i, n in enumerate(("ln_g", "ln_b", "b2")):
                sp.dma_start(rows[:, i].rearrange("p e n -> p (e n)"), d[n].partition_broadcast(P)).then_inc(rows_in, 16)
            store_x1(last)
            w.wait_ge(rows_in, 48)
            for e in range(E):
                w.wait_ge(w1_in[e], 16)
                sp.sem_inc(w1_ready, 1)
            for e in range(E):
                w.wait_ge(w2_in[e], 16)
                sp.sem_inc(w2_ready, 1)

        @block.tensor
        def _(pe):
            def job(bk, m, name, first, parts, rows=P, cols=COLS):
                bk.wait_empty(pe, m, name, first)
                out_ap = bk.tile(name)[0:rows, 0:cols]
                for i, (lhsT, rhs) in enumerate(parts):
                    mm = pe.matmul(out_ap, lhsT, rhs, start=(i == 0), stop=(i == len(parts) - 1))
                bk.fill(name, mm)

            def both(m, name, w, g, cols=None, rows=P):
                first = isinstance(m, int) and m == 0
                sl = cols
                parts = [] if first else [(w[:, k, sl], x_now[:, k]) for k in range(HALF)]
                parts += [(w[:, k, sl], bt(xm[g])[:, k]) for k in range(HALF)]
                ring.wait_empty(pe, m, name, first)
                o = ring.tile(name)[0:rows, :]
                for i, (lhsT, rhs) in enumerate(parts):
                    mm = pe.matmul(o.rearrange("p (b t) -> p b t", b=B), lhsT, rhs, start=(i == 0), stop=(i == len(parts) - 1))
                ring.fill(name, mm)

            def low(m, gs=range(4)):
                first = isinstance(m, int) and m == 0
                if gs[0] == 0:
                    mixed.wait(pe, m, "dx")
                    ring.wait_empty(pe, m, "lo1", first)
                    parts = [(w_maa1[:, k, :], x_now[:, k]) for k in range(HALF)]
                    parts += [(w_maa1x[:, k, :], bt(dx)[:, k]) for k in range(HALF)]
                    for i, (lhsT, rhs) in enumerate(parts):
                        mm = pe.matmul(ring.tile("lo1")[:, :].rearrange("p (b t) -> p b t", b=B), lhsT, rhs,
                                       start=(i == 0), stop=(i == len(parts) - 1))
                    ring.fill("lo1", mm)
                    lo_ok.wait(pe, m, "lo1")
                for g in gs:
                    for h in range(HALF):
                        job(ring, m, f"lo2_{g}{h}", first,
                            [(w_maa2[32 * g:32 * g + 32, h * P:(h + 1) * P], lo1[32 * g:32 * g + 32, :])])

            def sum_y(blk, s):
                q = blk * SLOTS + s
                pe.wait_ge(qm_ok, (q + 1) * Q_PARTS)
                first = isinstance(q, int) and q < SLOTS
                if s == 0 and not first:
                    post_act.wait(pe, blk - 1, "v1")
                elif s == 1 and not first:
                    tok.wait(pe, blk - 1, "z1")
                elif s == 2 and not first:
                    post_act.wait(pe, blk - 1, "lg")
                elif s:
                    pe.wait_ge(yr_ok, q)
                for j in range(HS):
                    mm = pe.matmul(y_sum, ident, Sh[:, s % 2, :, :, j], start=(j == 0), stop=(j == HS - 1))
                mm.then_inc(y_summed, 1)

            def project(m, y=None):
                first = False
                hs = lambda h: slice(h * P, (h + 1) * P)
                xm_ok.wait(pe, m, "11")
                both(m, "h1", w_h1, 1, cols=slice(0, 96), rows=96)
                xm_ok.wait(pe, m, "21")
                both(m, "h2", w_h2, 2, cols=slice(0, 64), rows=64)
                proj.wait(pe, m, "h1c")
                for h in range(HALF):
                    job(ring, m, f"z{h}", first, [(w_out1[:, 0, hs(h)], h1[0:96, :])])
                proj.wait(pe, m, "h2c")
                for h in range(HALF):
                    job(ring, m, f"mk{h}", first, [(w_out2[:, 1, hs(h)], h2[0:64, :])])
                both(m, "tg", w_gate1, 0, cols=slice(0, P))
                for h in range(HALF):
                    both(m, f"r{h}", w_sq[:, 0], 0, cols=hs(h))
                if y is not None:
                    sum_y(y, SLOTS - 1)
                for h in range(HALF):
                    both(m, f"k{h}", w_sq[:, 1], 2, cols=hs(h))
                xm_ok.wait(pe, m, "31")
                for h in range(HALF):
                    both(m, f"v{h}", w_sq[:, 2], 3, cols=hs(h))
                    if y is not None:
                        centre_y(y, h)
                for h in range(HALF):
                    if y is not None:
                        variance_y(y, h)
                    proj.wait(pe, m, f"k{h}")
                    job(ring, m, f"kk{h}", first, [(ident, kt[:, h]), (w_out2[:, 0, hs(h)], h2[0:64, :])])
                for h in range(HALF):
                    job(ring, m, f"a{h}", first, [(w_out1[:, 1, hs(h)], h1[0:96, :])])
                for h in range(HALF):
                    job(ring, m, f"ma{h}", first, [(w_out1[:, 2, hs(h)], h1[0:96, :])])
                proj.wait(pe, m, "sq1")
                for h in range(HALF):
                    job(ring, m, f"ss{h}", first, [(head_sum, nrm[:, h])])

            def gates(m):
                proj.wait(pe, m, "tg")
                for h in range(HALF):
                    job(ring, m, f"g{h}", False, [(w_gate2[:, h * P:(h + 1) * P], tg)])

            def bonus(m):
                comb.wait(pe, m, "rk1")
                for h in range(HALF):
                    job(ring, m, f"rk{h}", False, [(head_sum, rkt[:, h])])

            def centre_y(m, h):
                if h == 0:
                    pe.wait_ge(y_in, (m + 1) * 32)
                job(post, m, f"yc{h}", isinstance(m, int) and m == 0, [(centre, yc[:, h])])

            def variance_y(m, h):
                post_act.wait(pe, m, f"s{h}")
                job(post, m, f"var{h}", False, [(head_mean, ysq[:, h])])

            def norm(m):
                for h in range(HALF):
                    centre_y(m, h)
                for h in range(HALF):
                    variance_y(m, h)

            def project_out(m, w):
                post.wait_empty(pe, m, f"wo{w}", False)
                if not (isinstance(m, int) and m == last):
                    pe.wait_ge(yr_ok, (m + 1) * SLOTS + 1 + w)
                post_dve.wait(pe, m, "g1")
                for j in (2 * w, 2 * w + 1):
                    for h in range(HALF):
                        mm = pe.matmul(post.tile("wo0")[:, (j % 2) * C:(j % 2 + 1) * C], yc[:, h, j * P:(j + 1) * P],
                                       w_sq[:, 3, h, :], start=(h == 0), stop=(h == HALF - 1))
                post.fill(f"wo{w}", mm)

            def router(m):
                first = isinstance(m, int) and m == 0
                for w in range(2):
                    post.wait_empty(pe, m, f"xT{w}", first)
                    tok.wait(pe, m, "x1_3")
                    for q in range(4):
                        j, h = 2 * w + q // 2, q % 2
                        mm = pe.transpose(post.tile("xT0")[:, q * P:(q + 1) * P], xtok[:, j, h * P:(h + 1) * P], ident)
                    post.fill(f"xT{w}", mm)
                post.wait_empty(pe, m, "logit", first)
                post_act.wait(pe, m, "x1T1")
                x1q = x1T.rearrange("p h n -> p (h n)")
                for j in range(4):
                    for h in range(HALF):
                        mm = pe.matmul(post.tile("logit")[:, 8 * j:8 * j + 8], x1q[:, (2 * j + h) * P:(2 * j + h + 1) * P],
                                       cent[:, h, :], start=(h == 0), stop=(h == HALF - 1))
                post.fill("logit", mm)

            pe.wait_ge(early_in, 48)
            pe.wait_ge(const_ok, 9)
            low(0)
            pe.wait_ge(w_in, 16 * d["_nloads"])
            project(0)
            gates(0)
            bonus(0)
            low(1)

            def body(n, first, ahead):
                if ahead:
                    project(n + 1, None if first else n - 1)
                elif not first:
                    sum_y(n - 1, 3)
                    norm(n - 1)
                sum_y(n, 0)
                if ahead:
                    gates(n + 1)
                if not first:
                    project_out(n - 1, 0)
                if ahead:
                    bonus(n + 1)
                sum_y(n, 1)
                if not first:
                    project_out(n - 1, 1)
                    router(n - 1)
                if ahead == 2:
                    low(n + 2, (0, 1))
                sum_y(n, 2)
                if ahead == 2:
                    low(n + 2, (2, 3))

            body(0, True, 2)
            body(1, False, 2)
            with pe.Fori(2, last - 1) as n:
                body(n, False, 2)
            body(last - 1, False, 1)
            body(last, False, 0)
            sum_y(last, 3)
            norm(last)
            project_out(last, 0)
            project_out(last, 1)
            router(last)

            pe.wait_ge(route_in, 48)
            route.wait(pe, 0, "onehot")
            oh = onehot.rearrange("p n e -> p (n e)")
            pe.matmul(route_ps[0][:, 0:NTILE * E], tri, oh, start=True, stop=True)
            route_pe.inc("rank", pe.matmul(route_ps[1][:, 0:NTILE * E], all_ones, oh, start=True, stop=True))
            route.wait(pe, 0, "rows")
            for n in range(NTILE):
                pe.wait_ge(sel_ok, n // RSEL + 1)
                mm = pe.matmul(route_ps[2][:, 0:EBLK], in_slot[n // RSEL % 2][:, n % RSEL], in_blk[:, n],
                               start=(n == 0), stop=(n == NTILE - 1))
                if n % RSEL == RSEL - 1 and n < NTILE - 1:
                    mm.then_inc(sel_used, 1)
            route_pe.inc("table", mm)

            def turn_x(j, s):
                prep.wait(pe, j, "l")
                if not (isinstance(j, int) and j == 0):
                    xnT_ok.wait(pe, j - 1, "x")
                for k in range(HALF):
                    mm = pe.transpose(xnT_ps[:, k * P:(k + 1) * P], xn[:, k * P:(k + 1) * P], ident)
                turned_x.inc("x", mm)

            def expert_of(j):
                return pe.value_load(expert[0:1, bass.ds(j, 1)], min_val=0, max_val=E - 1)

            def first_layer(j):
                e = expert_of(j)
                xnT_ok.wait(pe, j, "x")
                if not (isinstance(j, int) and j == 0):
                    hid_ok.wait(pe, j - 1, "1")
                pe.wait_ge(w1_ready, e + 1)
                for i in range(2):
                    for k in range(HALF):
                        mm = pe.matmul(hid_ps[i][:, :], xnT[:, k, :],
                                       W1f[:, bass.ds(e * (HALF * F) + k * F + i * 512, 512)],
                                       start=(k == 0), stop=(k == HALF - 1))
                    first_mm.inc(str(i), mm)

            def turn_h(j):
                if not (isinstance(j, int) and j == 0):
                    relu_act.wait(pe, j - 1, str(FT // 2 - 1))
                    relu_dve.wait(pe, j - 1, str(FT - 1))
                hid_ok.wait(pe, j, "1")
                for t in range(FT):
                    mm = pe.transpose(hidT_ps[t // 4][:, (t % 4) * P:(t % 4 + 1) * P], hid[:, t * P:(t + 1) * P], ident)
                turned_h.inc("h", mm)

            def second_layer(j, s):
                e = expert_of(j)
                relu_act.wait(pe, j, str(FT // 2 - 1))
                relu_dve.wait(pe, j, str(FT - 1))
                if not (isinstance(j, int) and j < DEPTH):
                    fin.wait(pe, j - DEPTH, "z")
                pe.wait_ge(w2_ready, e + 1)
                for t in range(FT):
                    mm = pe.matmul(y_ps[s][:, 0:D], hidT[:, t, :], W2f[:, bass.ds(e * (FT * D) + t * D, D)],
                                   start=(t == 0), stop=(t == FT - 1))
                second_mm.inc("y", mm)

            W1f = view(at_proj, E * HALF * F)
            W2f = view(at_rec, E * FT * D)
            turn_x(0, 0)
            first_layer(0)
            turn_x(1, 1)

            def iteration(j, s):
                turn_h(j)
                if not (isinstance(j, int) and j + 1 >= EBLK):
                    first_layer(j + 1)
                second_layer(j, s)
                if not (isinstance(j, int) and j + 2 >= EBLK):
                    turn_x(j + 2, (s + 2) % DEPTH)

            for s in range(DEPTH):
                iteration(s, s)
            with pe.Fori(1, EBLK // DEPTH - 1) as i:
                for s in range(DEPTH):
                    iteration(i * DEPTH + s, s)
            for s in range(DEPTH):
                iteration(EBLK - DEPTH + s, s)

        @block.scalar
        def _(act):
            A = nc.scalar.activation

            def relay(q_blk, s):
                q = q_blk * SLOTS + s
                if s == 0:
                    act.wait_ge(pair_in, (q_blk + 1) * 80)
                p = s % 2
                zero = isinstance(q_blk, int) and q_blk == 0
                if not (zero and s < 2):
                    act.wait_ge(s_ok, (q - 1) * 32)
                    act.wait_ge(qm_ok, (q - 1) * Q_PARTS)
                t = slice(s * SUB, (s + 1) * SUB)
                if s == SLOTS - 1:
                    A(Wend, PA[:, :, TB], ACT.Copy)
                A(ab[p][:, 0], PA[:, :, t].rearrange("p c t -> p t c"), ACT.Copy)
                A(ab[p][:, 1], PX[:, 3, :, t].rearrange("p c t -> p t c"), ACT.Copy).then_inc(relayed, 1)
                A(kqv[:, p], PX[:, 0:3, :, t].rearrange("p x c t -> p x t c"), ACT.Copy).then_inc(relayed, 1)

            def low(m):
                ring.wait_full(act, m, "lo1")
                if not (isinstance(m, int) and m == 0):
                    ring.wait_full(act, m - 1, "ma1")
                lo_ok.inc("lo1", A(lo1, ring.tile("lo1")[:, :], ACT.Tanh))

            def evac(m, y=None):
                first = isinstance(m, int) and m == 0

                def ev(step, name, dst, func, rows=slice(0, P), **kw):
                    ins = A(dst, ring.tile(name)[rows, :], func, **kw)
                    proj.inc(step, ins)

                ring.wait_full(act, m, "h1")
                ev("h1t", "h1", h1[0:64, :], ACT.Tanh, slice(0, 64))
                ev("h1c", "h1", h1[64:96, :], ACT.Copy, slice(64, 96))
                ring.wait_full(act, m, "h2")
                ev("h2t", "h2", h2[0:32, :], ACT.Tanh, slice(0, 32))
                ev("h2c", "h2", h2[32:64, :], ACT.Copy, slice(32, 64))
                for h in range(HALF):
                    ring.wait_full(act, m, f"z{h}")
                    ev(f"z{h}", f"z{h}", zt[:, h], ACT.Identity, bias=prm("decay", h))
                    ev(f"abs{h}", f"z{h}", t1[:, h], ACT.Abs, bias=prm("decay", h))
                    proj.inc(f"sg{h}", A(sg[:, h], ring.tile(f"z{h}")[:, :], ACT.Sigmoid, bias=prm("decay", h)))
                for h in range(HALF):
                    ring.wait_full(act, m, f"mk{h}")
                    ev(f"mk{h}", f"mk{h}", mk[:, h], ACT.Sigmoid, bias=prm("misc_k", h))
                proj.wait(act, m, "abs1")
                proj.inc("exp", A(t1, t1, ACT.Exp, scale=-1.0))
                proj.wait(act, m, "exp")
                proj.inc("ln", A(t1, t1, ACT.Ln, bias=1.0))
                if not first:
                    ring.wait_full(act, m - 1, "g1")
                if not first:
                    relay(m - 1, 1)
                ring.wait_full(act, m, "tg")
                ev("tg", "tg", tg, ACT.Tanh)
                if not first:
                    act.wait_ge(scr_out, m * 160)
                    comb.wait(act, m - 1, "u1")
                for nm, dst in (("r", rt), ("k", kt), ("v", vt)):
                    for h in range(HALF):
                        ring.wait_full(act, m, f"{nm}{h}")
                        ev(f"{nm}{h}", f"{nm}{h}", dst[:, h], ACT.Copy)
                        if y is not None and nm == "v":
                            keep_centred(y, h)
                    if y is not None and nm == "r":
                        keep_y(y, SLOTS - 1, False)
                for h in range(HALF):
                    if y is not None:
                        keep_variance(y, h)
                    ring.wait_full(act, m, f"kk{h}")
                    ev(f"kk{h}", f"kk{h}", kk[:, h], ACT.Copy)
                    ev(f"sq{h}", f"kk{h}", nrm[:, h], ACT.Square)
                for h in range(HALF):
                    ring.wait_full(act, m, f"a{h}")
                    ev(f"a{h}", f"a{h}", at[:, h], ACT.Sigmoid, bias=prm("aaaaa", h))
                for h in range(HALF):
                    ring.wait_full(act, m, f"ma{h}")
                    ev(f"ma{h}", f"ma{h}", ma[:, h], ACT.Sigmoid, bias=prm("misc_a", h))
                    ev(f"nma{h}", f"ma{h}", nma[:, h], ACT.Sigmoid, bias=negp[:, h:h + 1], scale=-1.0)
                if not first:
                    relay(m - 1, 2)
                for h in range(HALF):
                    ring.wait_full(act, m, f"ss{h}")
                    ev(f"lnss{h}", f"ss{h}", nrm[:, h], ACT.Ln, bias=tiny)
                if y is not None:
                    log_variance(y)
                proj.wait(act, m, "lnss1")
                proj.inc("inv", A(nrm, nrm, ACT.Exp, scale=-0.5))
                if y is not None:
                    inverse_deviation(y)

            def keep_y(blk, s, first):
                q = blk * SLOTS + s
                if s == 0 and not first:
                    act.wait_ge(y_out, blk * 16)
                act.wait_ge(y_summed, q + 1)
                A(ysb[:, :, s * SUB:(s + 1) * SUB], y_sum.rearrange("p t i -> p i t"), ACT.Copy).then_inc(yr_ok, 1)

            def keep_centred(m, h):
                post.wait_full(act, m, f"yc{h}")
                post_act.inc(f"c{h}", A(yc[:, h], post.tile("yc0")[:, :], ACT.Copy))
                post_act.inc(f"s{h}", A(ysq[:, h], post.tile("yc0")[:, :], ACT.Square))

            def keep_variance(m, h):
                post.wait_full(act, m, f"var{h}")
                post_act.inc(f"v{h}", A(ysq[:, h], post.tile("var0")[:, :], ACT.Copy))

            def log_variance(m):
                post_act.wait(act, m, "v1")
                post_act.inc("ln", A(ysq, ysq, ACT.Ln, bias=gneps))

            def inverse_deviation(m):
                post_act.wait(act, m, "ln")
                post_act.inc("rstd", A(ysq, ysq, ACT.Exp, scale=-0.5))

            def norm_act(m):
                for h in range(HALF):
                    keep_centred(m, h)
                for h in range(HALF):
                    keep_variance(m, h)
                log_variance(m)
                inverse_deviation(m)

            def hand_over(m, first):
                if not first:
                    post_dve.wait(act, m - 1, "g1")
                comb_act.wait(act, m, "g1")
                handed.inc("gp", A(gp, gt, ACT.Copy))
                comb.wait(act, m, "u1")
                handed.inc("up", A(up, ut, ACT.Copy))

            def combine_act(m):
                comb.wait(act, m, f"scan{HALF - 1}")
                comb_act.inc("W", A(Wt[:, :, :, 1:TB + 1], bt(L), ACT.Exp, scale=-DECAY))
                comb_act.inc("iW", A(iW, L, ACT.Exp, scale=DECAY))
                comb.wait(act, m, "e2")
                comb_act.inc("ek", A(mk, mk, ACT.Exp))

            def gate_act(m):
                if not (isinstance(m, int) and m == 0):
                    handed.wait(act, m - 1, "gp")
                for h in range(HALF):
                    ring.wait_full(act, m, f"g{h}")
                    ins = A(gt[:, h], ring.tile(f"g{h}")[:, :], ACT.Copy)
                    comb_act.inc(f"g{h}", ins)

            def tok_std(m):
                tok.wait(act, m, "ag3")
                rst.inc("sqrt", A(std, mv[:, :, 1], ACT.Sqrt, bias=lneps))

            def x1T_act(m):
                for w in range(2):
                    post.wait_full(act, m, f"xT{w}")
                    ins = A(x1T[:, w], post.tile("xT0")[:, :], ACT.Copy)
                    post_act.inc(f"x1T{w}", ins)

            def keep_logits(m):
                post.wait_full(act, m, "logit")
                post_act.inc("lg", A(logits[:, bass.ds(m * 4, 4), :],
                                     post.tile("logit")[:, 0:32].rearrange("p (j e) -> p j e", e=8), ACT.Copy))

            act.wait_ge(early_in, 48)
            act.wait_ge(const_ok, 10)
            low(0)
            evac(0)
            combine_act(0)
            gate_act(0)
            low(1)
            relay(0, 0)

            def body(n, first, ahead):
                if ahead:
                    evac(n + 1, None if first else n - 1)
                elif not first:
                    relay(n, 1)
                    keep_y(n - 1, 3, False)
                    norm_act(n - 1)
                if not ahead:
                    relay(n, 2)
                if ahead:
                    combine_act(n + 1)
                keep_y(n, 0, first)
                relay(n, 3)
                hand_over(n, first)
                if ahead:
                    gate_act(n + 1)
                keep_y(n, 1, first)
                if not first:
                    tok_std(n - 1)
                    x1T_act(n - 1)
                    keep_logits(n - 1)
                if ahead == 2:
                    low(n + 2)
                if ahead:
                    relay(n + 1, 0)
                keep_y(n, 2, first)

            body(0, True, 2)
            with act.Fori(1, last - 1) as n:
                body(n, False, 2)
            body(last - 1, False, 1)
            body(last, False, 0)
            keep_y(last, 3, False)
            norm_act(last)
            tok_std(last)
            x1T_act(last)
            keep_logits(last)

            def expert_of(j):
                return act.value_load(expert[0:1, bass.ds(j, 1)], min_val=0, max_val=E - 1)

            def root(r, of_rows, of_results):
                if of_rows:
                    prep.wait(act, r, "ag")
                if of_results:
                    fin.wait(act, r - 3, "ag")
                w = slice(0 if of_rows else 1, 2 if of_results else 1)
                roots.inc("sqrt", A(estd[:, w], emv[:, w, 1], ACT.Sqrt, bias=lneps))

            def keep_hidden(j):
                if not (isinstance(j, int) and j == 0):
                    turned_h.wait(act, j - 1, "h")
                for i in range(2):
                    first_mm.wait(act, j, str(i))
                    hid_ok.inc(str(i), A(hid[:, i * 512:(i + 1) * 512], hid_ps[i][:, :], ACT.Copy))

            b1f = b1.rearrange("p e t -> p (e t)")

            def relu(j):
                e = expert_of(j)
                if not (isinstance(j, int) and j == 0):
                    second_mm.wait(act, j - 1, "y")
                turned_h.wait(act, j, "h")
                for t in range(FT // 2):
                    relu_act.inc(str(t), A(hidT[:, t], hidT_ps[0][:, t * P:(t + 1) * P], ACT.Relu,
                                           bias=b1f[:, bass.ds(e * FT + t, 1)]))

            route.wait(act, 0, "expert")
            root(0, True, False)
            root(1, True, False)
            keep_hidden(0)

            def iteration(j):
                known = isinstance(j, int)
                root(j + 2, not (known and j + 2 >= EBLK), not (known and j == 0))
                relu(j)
                if not (known and j + 1 >= EBLK):
                    keep_hidden(j + 1)

            for j in range(DEPTH):
                iteration(j)
            with act.Fori(1, EBLK // DEPTH - 1) as i:
                for s in range(DEPTH):
                    iteration(i * DEPTH + s)
            for j in range(EBLK - DEPTH, EBLK):
                iteration(j)
            root(EBLK + 2, False, True)

        @block.vector
        def _(dve):
            TT, STT = nc.vector.tensor_tensor, nc.vector.scalar_tensor_tensor
            nc.vector.memset(ones, 1.0).then_inc(const_ok, 1)
            nc.vector.memset(within, 1.0).then_inc(const_ok, 1)
            nc.vector.memset(tiny, TINY).then_inc(const_ok, 1)
            nc.vector.memset(gneps, GN_EPS).then_inc(const_ok, 1)
            nc.vector.memset(lneps, LN_EPS).then_inc(const_ok, 1)
            nc.vector.memset(Wt[:, :, :, 0:1], 1.0).then_inc(const_ok, 1)
            dve.wait_ge(early_in, 48)
            i = PARAMS.index("misc_a")
            nc.vector.tensor_scalar(negp, par[:, i, :], -1.0, None, ALU.mult).then_inc(const_ok, 1)
            for k in range(HALF):
                nc.vector.tensor_scalar(w_maa1x[:, k], w_maa1[:, k], prm("maa_x", k), None, ALU.mult).then_inc(const_ok, 1)
            dve.wait_ge(const_ok, 8 + 1)
            nc.vector.memset(within.rearrange("p (b t) -> p b t", b=B)[:, :, 0:1], 0.0).then_inc(const_ok, 1)
            dve.wait_ge(const_ok, 8 + 2)

            def mix_stage(m):
                dve.wait_ge(xT_in, (m + 1) * 32)
                if not (isinstance(m, int) and m == 0):
                    comb.wait(dve, m - 1, "e2")
                    ring.wait_full(dve, m - 1, "v1")
                mixed.inc("dx", TT(bt(dx), x_prev, x_now, ALU.subtract))

            def xm_stage(m):
                if not (isinstance(m, int) and m == 0):
                    ring.wait_full(dve, m - 1, "rk1")
                    comb_act.wait(dve, m - 1, "iW")
                    comb.wait(dve, m - 1, "u1")
                    comb_pool.wait(dve, m - 1, "q")
                for g in range(4):
                    for h in range(HALF):
                        nm = f"lo2_{g}{h}"
                        ring.wait_full(dve, m, nm)
                        ins = STT(out=xm[g][:, h], in0=ring.tile(nm)[:, :], scalar=prm(f"maa{g}", h), in1=dx[:, h],
                                  op0=ALU.add, op1=ALU.mult)
                        if isinstance(m, int) and m == 0:
                            ins.then_inc(with_x, 1)
                            dve.wait_ge(with_x, 2 * g + h + 1)
                            ins = TT(bt(xm[g])[:, h], bt(xm[g])[:, h], x_now[:, h], ALU.add)
                        xm_ok.inc(f"{g}{h}", ins)

            def decays(m):
                first = isinstance(m, int) and m == 0

                def do(step, ins):
                    comb.inc(step, ins)

                def after(step):
                    comb.wait(dve, m, step)

                proj.wait(dve, m, "ln")
                do("ls", STT(out=zt, in0=zt, scalar=0.0, in1=t1, op0=ALU.min, op1=ALU.subtract))
                after("ls")
                do("e2", STT(out=mk, in0=zt, scalar=-0.5, in1=mk, op0=ALU.add, op1=ALU.mult))
                ring.wait_full(dve, m, "r1")
                for h in range(HALF):
                    do(f"scan{h}", nc.vector.tensor_tensor_scan(L[:, h], within, sg[:, h], 0.0, ALU.mult, ALU.add))

            def combine(m):
                first = isinstance(m, int) and m == 0

                def do(step, ins):
                    comb.inc(step, ins)

                def after(step):
                    comb.wait(dve, m, step)

                proj.wait(dve, m, "inv")
                do("kkn", STT(out=kk, in0=nrm, scalar=1e12, in1=kk, op0=ALU.min, op1=ALU.mult))
                do("t", TT(nma, at, nma, ALU.mult))
                after("kkn")
                after("t")
                do("bt", STT(out=at, in0=kk, scalar=-1.0, in1=at, op0=ALU.mult, op1=ALU.mult))
                do("f", TT(ma, nma, ma, ALU.add))
                after("f")
                do("k2", TT(kt, ma, kt, ALU.mult))
                comb_act.wait(dve, m, "ek")
                after("k2")
                do("k3", TT(kt, kt, mk, ALU.mult))
                after("k3")
                for h in range(HALF):
                    do(f"rk{h}", STT(out=rkt[:, h], in0=rt[:, h], scalar=prm("faaaa", h), in1=kt[:, h],
                                     op0=ALU.mult, op1=ALU.mult))
                do("aend", nc.vector.tensor_copy(ao[:, :, :, TB:TB + 1], Wt[:, :, :, TB:TB + 1]))
                after("rk1")
                do("k", TT(kt, kt, iW, ALU.mult))
                if not first:
                    handed.wait(dve, m - 1, "up")
                for h in range(HALF):
                    ring.wait_full(dve, m, f"rk{h}")
                    ins = TT(ut[:, h], ring.tile(f"rk{h}")[:, :], vt[:, h], ALU.mult)
                    do(f"u{h}", ins)

            def normed(m):
                post_act.wait(dve, m, "rstd")
                post_dve.inc("n", TT(yc, yc, ysq, ALU.mult))
                handed.wait(dve, m, "up")
                post_dve.wait(dve, m, "n")
                for h in range(HALF):
                    post_dve.inc(f"w{h}", STT(out=yc[:, h], in0=yc[:, h], scalar=prm("ln_w", h), in1=up[:, h],
                                              op0=ALU.mult, op1=ALU.add))
                for h in range(HALF):
                    post_dve.wait(dve, m, f"w{h}")
                    post_dve.inc(f"g{h}", STT(out=yc[:, h], in0=yc[:, h], scalar=prm("ln_b", h), in1=gp[:, h],
                                              op0=ALU.add, op1=ALU.mult))

            def add_tokens(m, tiles):
                dve.wait_ge(xtok_in, (m + 1) * 32)
                for j in tiles:
                    w = f"wo{j // 2}"
                    post.wait_full(dve, m, w)
                    tok.inc(f"z{j}", TT(xtok[:, j], xtok[:, j], post.tile(w)[:, (j % 2) * C:(j % 2 + 1) * C], ALU.add))

            def tokens(m):
                for j in range(4):
                    tok.wait(dve, m, f"z{j}")
                    tok.inc(f"st{j}", nc.vector.bn_stats(stats[:, j], xtok[:, j]))
                tok.wait(dve, m, "st3")
                tok.inc("settle", nc.vector.memset(spare, 0.0))
                for j in range(4):
                    tok.inc(f"ag{j}", nc.vector.bn_aggr(mv[:, j], stats[:, j]))
                rst.wait(dve, m, "sqrt")
                tok.inc("inv", nc.vector.reciprocal(std, std))
                tok.wait(dve, m, "inv")
                for j in range(4):
                    tok.inc(f"x1_{j}", nc.vector.tensor_scalar(xtok[:, j], xtok[:, j], mv[:, j, 0:1], std[:, j:j + 1],
                                                               ALU.subtract, ALU.mult))

            def hv(ap, h):
                return ap[:, 8 * h:8 * h + 8, :]

            def start_slot(blk, s, first):
                q = blk * SLOTS + s
                if first and s == 0:
                    nc.vector.memset(S0, 0.0).then_inc(s0_ok, 1)
                    return
                dve.wait_ge(s_ok, q * 32)
                prev = Sh[:, (s - 1) % 2, SUB - 1]
                if s == 0:
                    nc.vector.tensor_tensor(S0, prev, Wend[:, None, :].broadcast_to([P, HS, HS]), ALU.mult).then_inc(s0_ok, 1)
                else:
                    nc.vector.tensor_copy(S0, prev).then_inc(s0_ok, 1)

            def steps(blk, s, first):
                q = blk * SLOTS + s
                p = s % 2
                dve.wait_ge(relayed, (q + 1) * 2)
                for t in range(SUB):
                    prev = S0 if t == 0 else Sh[:, p, t - 1]
                    a = ab[p][:, 0, t, None, :].broadcast_to([P, 8, HS])
                    b = ab[p][:, 1, t, None, :].broadcast_to([P, 8, HS])
                    for h in range(2):
                        if t == 0:
                            dve.wait_ge(s0_ok, q + 1)
                        else:
                            dve.wait_ge(s_ok, q * 32 + 2 * (t - 1) + h + 1)
                        TT(hv(M, h), hv(prev, h), a, ALU.mult).then_inc(chain, 1)
                    for h in range(2):
                        dve.wait_ge(chain, q * 96 + t * 6 + h + 1)
                        nc.vector.tensor_reduce(SA[:, 8 * h:8 * h + 8], hv(M, h), AX.X, ALU.add).then_inc(chain, 1)
                    for h in range(2):
                        dve.wait_ge(chain, q * 96 + t * 6 + h + 3)
                        TT(hv(outer, h), SA[:, 8 * h:8 * h + 8, None].broadcast_to([P, 8, HS]), b, ALU.mult).then_inc(chain, 1)
                    dve.wait_ge(z_ok, q * SUB + t + 1)
                    if t == 0 and not (first and s < 2):
                        dve.wait_ge(y_summed, q - 1)
                    for h in range(2):
                        dve.wait_ge(chain, q * 96 + t * 6 + h + 5)
                        TT(hv(Sh[:, p, t], h), hv(outer, h), hv(Z[:, t % 2], h), ALU.add).then_inc(s_ok, 1)

            mix_stage(0)
            xm_stage(0)
            decays(0)
            combine(0)
            mix_stage(1)

            def body(n, first, ahead):
                start_slot(n, 0, first)
                if ahead:
                    xm_stage(n + 1)
                steps(n, 0, first)
                start_slot(n, 1, False)
                if ahead:
                    decays(n + 1)
                steps(n, 1, first)
                start_slot(n, 2, False)
                if ahead == 2:
                    mix_stage(n + 2)
                if not first:
                    normed(n - 1)
                if ahead:
                    combine(n + 1)
                if not first:
                    add_tokens(n - 1, (0, 1))
                steps(n, 2, first)
                start_slot(n, 3, False)
                if not first:
                    add_tokens(n - 1, (2, 3))
                    tokens(n - 1)
                steps(n, 3, first)

            body(0, True, 2)
            with dve.Fori(1, last - 1) as n:
                body(n, False, 2)
            body(last - 1, False, 1)
            body(last, False, 0)
            dve.wait_ge(s_ok, NBLK * SLOTS * 32)
            for t, k in Q_BEFORE[1:] + list(Q_BETWEEN.values()):
                q = kqv[:, 1, 1, t:t + k, None, :].broadcast_to([P, k, HS, HS])
                TT(Sh[:, 1, t:t + k], Sh[:, 1, t:t + k], q, ALU.mult).then_inc(qm_ok, 1)
            normed(last)
            add_tokens(last, range(4))
            tokens(last)

            dve.wait_ge(route_in, 48)
            R = lambda name: route.wait(dve, 0, name)
            post_act.wait(dve, last, "lg")
            red = nc.vector.tensor_reduce
            b3 = lambda ap: ap[:, :, None].broadcast_to([P, NTILE, E])
            route.inc("max", red(best, logits, AX.X, ALU.max))
            R("max")
            route.inc("eq", TT(onehot, logits, b3(best), ALU.is_ge))
            R("eq")
            route.inc("code", TT(onehot, onehot, cst["prefer"][:, None, :].broadcast_to([P, NTILE, E]), ALU.mult))
            R("code")
            route.inc("cmax", red(best, onehot, AX.X, ALU.max))
            R("cmax")
            route.inc("onehot", TT(onehot, onehot, b3(best), ALU.is_equal))
            route_pe.wait(dve, 0, "rank")
            rank = ne(route_ps[0][:, 0:NTILE * E])
            totals = route_ps[1][:, 0:NTILE * E].rearrange("p (n e) -> p e n", e=E)
            route.inc("sum", nc.vector.tensor_copy(place, rank))
            for e in range(E):
                route.inc(f"run{e}", nc.vector.tensor_tensor_scan(run[:, e], ones[:, 0:NTILE], totals[:, e], 0.0, ALU.mult, ALU.add))
            R(f"run{E - 1}")
            c2 = cmp[:, 0:E * NTILE].rearrange("p (e n) -> p e n", e=E)
            route.inc("cnt", TT(c2, run[:, :, NTILE - 1:NTILE].broadcast_to([P, E, NTILE]),
                                cst["fill"][:, None, :].broadcast_to([P, E, NTILE]), ALU.is_gt))
            R("cnt")
            route.inc("nblk", red(blocks, c2, AX.X, ALU.add))
            R("nblk")
            route.inc("bend", nc.vector.tensor_tensor_scan(blk_end, ones[:, 0:E], blocks, 0.0, ALU.mult, ALU.add))
            R("bend")
            route.inc("bstart", TT(blocks, blk_end, blocks, ALU.subtract))
            route.inc("excl", TT(run, run, totals, ALU.subtract))
            R("excl")
            route.inc("p1", TT(place, place, run.rearrange("p e n -> p n e"), ALU.add))
            R("p1")
            route.inc("p2", STT(out=place, in0=blocks[:, None, :].broadcast_to([P, NTILE, E]), scalar=float(P), in1=place,
                                op0=ALU.mult, op1=ALU.add))
            R("p2")
            route.inc("p3", TT(place, place, onehot, ALU.mult))
            R("p3")
            route.inc("pos", red(posf, place, AX.X, ALU.add))
            R("pos")
            route.inc("posi", nc.vector.tensor_copy(posi, posf))
            R("posi")
            route.inc("slot", nc.vector.tensor_scalar(slotp, posi, P - 1, None, ALU.bitwise_and))
            route.inc("blk", nc.vector.tensor_scalar(blki, posi, P.bit_length() - 1, None, ALU.logical_shift_right))
            R("blk")
            route.inc("slotf", nc.vector.tensor_copy(slotf, slotp))
            route.inc("blkf", nc.vector.tensor_copy(blkf, blki))
            c3 = cmp[:, 0:EBLK * E].rearrange("p (j e) -> p j e", e=E)
            route.inc("ecmp", TT(c3, cst["eblock"][:, :, None].broadcast_to([P, EBLK, E]),
                                 blk_end[:, None, :].broadcast_to([P, EBLK, E]), ALU.is_ge))
            R("ecmp")
            route.inc("esum", red(efl, c3, AX.X, ALU.add))
            R("esum")
            route.inc("expert", nc.vector.tensor_scalar(expert, efl, float(E - 1), None, ALU.min))
            wide = [P, NTILE, EBLK]
            route.inc("inblk", TT(in_blk, cst["eblock"][:, None, :].broadcast_to(wide), blkf[:, :, None].broadcast_to(wide),
                                  ALU.is_equal))
            R("inblk")
            route.inc("rows", TT(in_blk, in_blk, cst["row"][:, :, None].broadcast_to(wide), ALU.mult))
            for g in range(NTILE // RSEL):
                if g >= 2:
                    dve.wait_ge(sel_used, g - 1)
                some = [P, RSEL, P]
                TT(in_slot[g % 2], cst["slot"][:, None, :].broadcast_to(some),
                   slotf[:, g * RSEL:(g + 1) * RSEL, None].broadcast_to(some), ALU.is_equal).then_inc(sel_ok, 1)
            route_pe.wait(dve, 0, "table")
            nc.vector.tensor_scalar(table, route_ps[2][:, 0:EBLK], float(NTOK), None, ALU.add).then_inc(table_ok, 1)

            def expert_of(j):
                return dve.value_load(expert[0:1, bass.ds(j, 1)], min_val=0, max_val=E - 1)

            def row(w, e):
                return view(at_rows + w * E * D, E * D)[:, bass.ds(e * D, D)]

            def prepare_stats(j, s):
                if isinstance(j, int):
                    dve.wait_ge(gathered[s], 16 * (j // DEPTH + 1))
                else:
                    dve.wait_ge(gathered[s], round_of(j, s) * 16)
                prep.inc("st", nc.vector.bn_stats(estat[:, 0], xg[:, s]))
                prep.wait(dve, j, "st")
                prep.inc("settle", nc.vector.memset(spare, 0.0))
                prep.inc("ag", nc.vector.bn_aggr(emv[:, 0], estat[:, 0]))

            def prepare(j, s):
                known = isinstance(j, int)
                e = expert_of(j)
                if not (known and j == 0):
                    turned_x.wait(dve, j - 1, "x")
                inverse.wait(dve, j, "inv")
                prep.inc("xh", nc.vector.tensor_scalar(xn, xg[:, s], emv[:, 0, 0:1], estd[:, 0:1], ALU.subtract, ALU.mult))
                prep.wait(dve, j, "xh")
                prep.inc("g", TT(xn, xn, row(0, e), ALU.mult))
                prep.wait(dve, j, "g")
                prep.inc("l", TT(xn, xn, row(1, e), ALU.add))
                prep.inc("zb", STT(out=zb[:, s], in0=xg[:, s], scalar=2.0, in1=row(2, e), op0=ALU.mult, op1=ALU.add))

            def keep_xnT(j):
                if not (isinstance(j, int) and j == 0):
                    first_mm.wait(dve, j - 1, "1")
                turned_x.wait(dve, j, "x")
                xnT_ok.inc("x", nc.vector.tensor_copy(xnT, xnT_ps[:, 0:D].rearrange("p (k n) -> p k n", k=HALF)))

            b1f = b1.rearrange("p e t -> p (e t)")

            def relu(j):
                e = expert_of(j)
                if not (isinstance(j, int) and j == 0):
                    second_mm.wait(dve, j - 1, "y")
                turned_h.wait(dve, j, "h")
                for t in range(FT // 2, FT):
                    relu_dve.inc(str(t), nc.vector.tensor_scalar(hidT[:, t], hidT_ps[1][:, (t - 4) * P:(t - 3) * P],
                                                                 b1f[:, bass.ds(e * FT + t, 1)], 0.0, ALU.add, ALU.max))

            def finish_stats(j, s):
                second_mm.wait(dve, j, "y")
                fin.inc("z", TT(zb[:, s], zb[:, s], y_ps[s][:, 0:D], ALU.add))
                fin.wait(dve, j, "z")
                fin.inc("st", nc.vector.bn_stats(estat[:, 1], zb[:, s]))
                fin.wait(dve, j, "st")
                fin.inc("settle", nc.vector.memset(spare, 0.0))
                fin.inc("ag", nc.vector.bn_aggr(emv[:, 1], estat[:, 1]))

            def finish(j, s):
                if not (isinstance(j, int) and j < DEPTH):
                    dve.wait_ge(scattered[s], (round_of(j, s) - 1) * 16)
                inverse.wait(dve, j + 3, "inv")
                fin.inc("o", nc.vector.tensor_scalar(ob[:, s], zb[:, s], emv[:, 1, 0:1], estd[:, 1:2], ALU.subtract, ALU.mult))

            def invert(r, of_rows, of_results):
                roots.wait(dve, r, "sqrt")
                w = slice(0 if of_rows else 1, 2 if of_results else 1)
                inverse.inc("inv", nc.vector.reciprocal(estd[:, w], estd[:, w]))

            rounds = {}

            def round_of(j, s):
                return j // DEPTH + 1 if isinstance(j, int) else rounds[0] + (j_off[0] // DEPTH) + 1

            j_off = [0]
            dve.wait_ge(rows_in, 48)
            prepare_stats(0, 0)
            invert(0, True, False)
            prepare(0, 0)
            keep_xnT(0)
            prepare_stats(1, 1)
            invert(1, True, False)
            prepare(1, 1)
            keep_xnT(1)

            def iteration(j, s, i=None):
                rounds[0] = i
                known = isinstance(j, int)
                if not (known and j == 0):
                    finish_stats(j - 1, (s - 1) % DEPTH)
                if not (known and j + 2 >= EBLK):
                    j_off[0] = s + 2
                    prepare_stats(j + 2, (s + 2) % DEPTH)
                relu(j)
                invert(j + 2, not (known and j + 2 >= EBLK), not (known and j == 0))
                if not (known and j == 0):
                    j_off[0] = s - 1 if s else -1
                    finish(j - 1, (s - 1) % DEPTH)
                if not (known and j + 2 >= EBLK):
                    prepare(j + 2, (s + 2) % DEPTH)
                    keep_xnT(j + 2)

            for j in range(2 * DEPTH):
                iteration(j, j % DEPTH)
            with dve.Fori(2, EBLK // DEPTH - 1) as i:
                for s in range(DEPTH):
                    iteration(i * DEPTH + s, s, i)
            for s in range(DEPTH):
                iteration(EBLK - DEPTH + s, s)
            finish_stats(EBLK - 1, DEPTH - 1)
            invert(EBLK + 2, False, True)
            finish(EBLK - 1, DEPTH - 1)

        @block.gpsimd
        def _(pool):
            TT = nc.gpsimd.tensor_tensor

            def outer_vk(s, t):
                p = s % 2
                k = kqv[:, p, 0, t, None, :].broadcast_to([P, HS, HS])
                v = kqv[:, p, 2, t, :, None].broadcast_to([P, HS, HS])
                TT(VK[:, t % 8], v, k, ALU.mult).then_inc(vk_ok, 1)

            def times_q(s, parts):
                p = s % 2
                for t, n in parts:
                    q = kqv[:, p, 1, t:t + n, None, :].broadcast_to([P, n, HS, HS])
                    TT(Sh[:, p, t:t + n], Sh[:, p, t:t + n], q, ALU.mult).then_inc(qm_ok, 1)

            def combine_pool(m):
                comb.wait(pool, m, "kkn")
                comb_act.wait(pool, m, "iW")
                comb_pool.inc("ao", TT(ao[:, :, :, 0:TB], bt(kk), Wt[:, :, :, 0:TB], ALU.mult))
                comb.wait(pool, m, "bt")
                comb_pool.inc("b", TT(at, at, iW, ALU.mult))
                comb.wait(pool, m, "rk1")
                comb_pool.inc("q", TT(bt(rt), bt(rt), Wt[:, :, :, 1:TB + 1], ALU.mult))

            def slot(blk, s, first, ahead):
                q = blk * SLOTS + s
                if first and s == 0:
                    pool.wait_ge(relayed, 2)
                    for t in range(4):
                        outer_vk(0, t)
                pool.wait_ge(s0_ok, q + 1)
                if not (first and s == 0):
                    times_q((s - 1) % SLOTS, Q_BEFORE + (list(Q_BETWEEN.values()) if s == 2 else []))
                if s == 2 and ahead:
                    combine_pool(blk + 1)
                for t in range(SUB):
                    pool.wait_ge(vk_ok, q * SUB + t + 1)
                    if t:
                        pool.wait_ge(s_ok, q * 32 + 2 * t)
                    TT(Z[:, t % 2], S0 if t == 0 else Sh[:, s % 2, t - 1], VK[:, t % 8], ALU.add).then_inc(z_ok, 1)
                    if t in Q_BETWEEN and s != 2 and not (first and s == 0):
                        times_q((s - 1) % SLOTS, [Q_BETWEEN[t]])
                    if t < 12:
                        outer_vk(s, t + 4)
                    elif ahead or s < 3:
                        if t == 12:
                            pool.wait_ge(relayed, (q + 2) * 2)
                        outer_vk((s + 1) % SLOTS, t - 12)

            combine_pool(0)
            for s in range(SLOTS):
                slot(0, s, True, True)
            with pool.Fori(1, last) as n:
                for s in range(SLOTS):
                    slot(n, s, False, True)
            for s in range(SLOTS):
                slot(last, s, False, False)
            pool.wait_ge(s_ok, NBLK * SLOTS * 32)
            times_q(3, Q_BEFORE[:1])

            x_rows = x1d.rearrange("b t c -> (b t) c")
            out_rows = out.rearrange("b t c -> (b t) c")
            pool.wait_ge(table_ok, 1)
            pool.wait_ge(x1_out, NBLK * 32)
            nc.gpsimd.memset(xg, 0.0).then_inc(xg_clear, 1)
            pool.wait_ge(xg_clear, 1)

            w = Waits(pool, carrier_pool)

            def gather(j, s):
                if not (isinstance(j, int) and j < DEPTH):
                    prep.wait(w, j - DEPTH, "zb")
                idx_ok.inc("gather", nc.gpsimd.tensor_copy(gidx[:, s:s + 1], table[:, bass.ds(j, 1)]))
                idx_ok.wait(w, j, "gather")
                nc.gpsimd.indirect_dma_start(out=xg[:, s], out_offset=None, in_=x_rows,
                                             in_offset=bass.IndirectOffsetOnAxis(ap=gidx[:, s:s + 1], axis=0),
                                             bounds_check=NTOK - 1, oob_is_err=False).then_inc(gathered[s], 16)

            def scatter(j, s):
                fin.wait(w, j, "o")
                sidx_ok.inc("scatter", nc.gpsimd.tensor_copy(sidx[:, s:s + 1], table[:, bass.ds(j, 1)]))
                sidx_ok.wait(w, j, "scatter")
                nc.gpsimd.indirect_dma_start(out=out_rows, out_offset=bass.IndirectOffsetOnAxis(ap=sidx[:, s:s + 1], axis=0),
                                             in_=ob[:, s], in_offset=None,
                                             bounds_check=NTOK - 1, oob_is_err=False).then_inc(scattered[s], 16)

            for s in range(DEPTH):
                gather(s, s)

            def iteration(j, s):
                if not (isinstance(j, int) and j + DEPTH >= EBLK):
                    gather(j + DEPTH, s)
                if not (isinstance(j, int) and j == 0):
                    scatter(j - 1, (s - 1) % DEPTH)

            for s in range(DEPTH):
                iteration(s, s)
            with pool.Fori(1, EBLK // DEPTH - 1) as i:
                for s in range(DEPTH):
                    iteration(i * DEPTH + s, s)
            for s in range(DEPTH):
                iteration(EBLK - DEPTH + s, s)
            scatter(EBLK - 1, DEPTH - 1)
            for s in range(DEPTH):
                pool.wait_ge(scattered[s], EBLK // DEPTH * 16)


def layout(inputs):
    import numpy as np
    g = {k[len("L0_attn_"):]: np.asarray(v) for k, v in inputs.items() if k.startswith("L0_attn_")}
    f = {k[len("L0_ffn_"):]: np.asarray(v) for k, v in inputs.items() if k.startswith("L0_ffn_")}
    xTp = np.zeros((C, B, T + 1), np.float32)
    xTp[:, :, 1:] = g["x"].transpose(2, 0, 1)
    out1 = np.zeros((3, 96, C), np.float32)
    out1[0, 0:64], out1[1, 64:80], out1[2, 80:96] = g["decay_w2"], g["aaa_w2"], g["ma_w2"]
    out2 = np.zeros((2, 64, C), np.float32)
    out2[0, 0:16], out2[1, 32:48] = g["kkk_w2"], g["mk_w2"]
    h2T = np.zeros((C, 64), np.float32)
    h2T[:, 0:16], h2T[:, 32:48] = g["kkk_w1"].T, g["mk_w1"].T
    i = np.arange(P)
    same = (i[:, None] // HS == i[None, :] // HS).astype(np.float32)
    eye = np.eye(P, dtype=np.float32)
    cc = np.ascontiguousarray
    tile, part = np.arange(NTILE)[None, :], i[:, None]
    row = (2 * (tile % 4) + part // TB) * T + (tile // 4) * TB + part % TB
    wide = lambda v: np.broadcast_to(np.asarray(v)[None, :], (P, len(v)))
    cst = {"slot": wide(np.arange(P)), "eblock": wide(np.arange(EBLK)), "prefer": wide(E - np.arange(E)),
           "fill": wide(P * np.arange(NTILE)), "row": row - NTOK}
    return {
        "x": cc(g["x"]), "xTp": xTp,
        "WrT": cc(g["Wr"].T), "WkT": cc(g["Wk"].T), "WvT": cc(g["Wv"].T), "WoT": cc(g["Wo"].T),
        "maa1T": cc(g["maa_w1"].T), "maa2": cc(g["maa_w2"].reshape(P, C)),
        "gate1T": cc(g["gate_w1"].T), "gate2": cc(g["gate_w2"]),
        "h1T": cc(np.concatenate([g["decay_w1"].T, g["aaa_w1"].T, g["ma_w1"].T], axis=1)), "h2T": h2T,
        "out1": out1, "out2": out2,
        "mats": np.stack([same, same / HS, eye - same / HS, eye]).astype(np.float32),
        "centT": cc(f["centroids"].T),
        "mats2": np.stack([i[:, None] < i[None, :], np.ones((P, P), bool)]).astype(np.float32),
        "cst": np.concatenate([cst[n] for n in CONSTS], axis=1).astype(np.float32),
        "W1": cc(f["W1"]), "W2": cc(f["W2"]), "b1T": cc(f["b1"].reshape(E * FT, P).T),
        "ln_g": cc(f["ln_g"].reshape(-1)), "ln_b": cc(f["ln_b"].reshape(-1)), "b2": cc(f["b2"].reshape(-1)),
        "par": cc(np.stack([g["time_maa_x"]] + [g["time_maa"].reshape(4, C)[k] for k in range(4)]
                           + [g["time_decay"], g["time_aaaaa"], g["time_misc_a"], g["time_misc_k"], g["time_faaaa"],
                              g["ln_w"], g["ln_b"]]).reshape(len(PARAMS), HALF, P).transpose(2, 0, 1)),
    }


def kernel(**inputs):
    import concourse.bacc as bacc
    from concourse.bass_utils import run_bass_kernel_spmd as run

    nc = bacc.Bacc("TRN2", target_bir_lowering=False, num_devices=1)
    arrays = layout(inputs)
    d = {n: nc.dram_tensor(f"in_{n}", a.shape, mybir.dt.from_np(a.dtype), kind="ExternalInput").ap() for n, a in arrays.items()}
    d["_nloads"] = 12
    out = nc.dram_tensor("out_0_dram", (B, T, C), F32, kind="ExternalOutput").ap()
    build(nc, d, out)
    r = run(nc, [{f"in_{n}": a for n, a in arrays.items()}], core_ids=[0])
    return r.results[0]["out_0_dram"]
```
